# Optimizing a Trainium2 kernel written in Bass

```python
import numpy as np
import jax
import jax.numpy as jnp

def _softmax(x, axis=-1):
    return jax.nn.softmax(x, axis=axis)

def _gelu(x):
    return jax.nn.gelu(x, approximate=True)

def _silu(x):
    return jax.nn.silu(x)

def _sigmoid(x):
    return jax.nn.sigmoid(x)

def _layernorm(x, axis=-1, eps=1e-05):
    m = jnp.mean(x, axis=axis, keepdims=True)
    v = jnp.var(x, axis=axis, keepdims=True)
    return (x - m) / jnp.sqrt(v + eps)

def _scatter_add(tgt, idx, src, axis=0):
    return tgt.at[idx].add(src)

def _segment_sum(src, seg, n):
    return jax.ops.segment_sum(src, seg, n)
kernel_name = 'mk_vit_tower_postln_d1_tok_img1024_r4_00a3bc'

def setup_inputs(seed: int=0):
    np.random.seed(seed)
    _w = jnp.asarray

    def _rec_inputs():
        import jax
        import jax.numpy as jnp
        _rk = jax.random.key(seed)
        x = -0.00016672 + 0.999947 * jax.random.normal(jax.random.fold_in(_rk, 1), (64, 3, 96, 96), jnp.float32)
        return x
    x = _rec_inputs()

    def _L0_tok_setup():
        import jax, jax.numpy as jnp
        import numpy as np
        IMG = 96
        PATCH = 16
        C_IN = 3
        EMBED = 256
        NPH = IMG // PATCH
        NUM_PATCHES = NPH * NPH
        PATCH_DIM = PATCH * PATCH * C_IN
        key = jax.random.key(seed)
        k_x, k_w, k_b, k_cls, k_pos = jax.random.split(key, 5)
        x = jax.random.normal(k_x, (64, C_IN, IMG, IMG), dtype=jnp.float32)
        W = jax.random.normal(k_w, (EMBED, PATCH_DIM), dtype=jnp.float32) * (1.0 / np.sqrt(PATCH_DIM))
        b = jax.random.normal(k_b, (EMBED,), dtype=jnp.float32) * 0.01
        cls_token = jax.random.normal(k_cls, (1, 1, EMBED), dtype=jnp.float32) * 0.02
        pos_embed = jax.random.normal(k_pos, (1, NUM_PATCHES + 1, EMBED), dtype=jnp.float32) * 0.02
        return {'x': x, 'W': W, 'b': b, 'cls_token': cls_token, 'pos_embed': pos_embed}
    _L0_tok_all = _L0_tok_setup()
    _L0_tok_in = {k: v for k, v in _L0_tok_all.items() if k in ('W', 'b', 'cls_token', 'pos_embed')}
    del _L0_tok_all

    def _L0_attn_setup():
        import jax, jax.numpy as jnp
        import numpy as np
        HEADS = 16
        DIM_HEAD = 64
        T_MAX = DIM_HEAD

        def _cope(q, sim, pos_emb):
            G = jax.nn.sigmoid(sim)
            P = jnp.flip(jnp.cumsum(jnp.flip(G, axis=-1), axis=-1), axis=-1)
            P = jnp.minimum(P, T_MAX - 1)
            P_floor = jnp.floor(P)
            P_ceil_i = jnp.ceil(P).astype(jnp.int32)
            P_floor_i = P_floor.astype(jnp.int32)
            E = jnp.einsum('bnc,ct->bnt', q, pos_emb)
            E_ceil = jnp.take_along_axis(E, P_ceil_i, axis=-1)
            E_floor = jnp.take_along_axis(E, P_floor_i, axis=-1)
            w = P - P_floor
            return w * E_ceil + (1.0 - w) * E_floor
        key = jax.random.key(seed)
        ks = jax.random.split(key, 6)
        B, N, D = (1, 512, 256)
        inner = HEADS * DIM_HEAD
        return {'x': jax.random.normal(ks[0], (B, N, D), dtype=jnp.float32), 'Wq': jax.random.normal(ks[1], (D, inner), dtype=jnp.float32) * 0.02, 'Wkv': jax.random.normal(ks[2], (D, 2 * inner), dtype=jnp.float32) * 0.02, 'Wout': jax.random.normal(ks[3], (inner, D), dtype=jnp.float32) * 0.02, 'b_out': jnp.zeros((D,), dtype=jnp.float32), 'pos_emb': jax.random.normal(ks[4], (DIM_HEAD, T_MAX), dtype=jnp.float32) * 0.02}
    _L0_attn_all = _L0_attn_setup()
    _L0_attn_in = {k: v for k, v in _L0_attn_all.items() if k in ('Wq', 'Wkv', 'Wout', 'b_out', 'pos_emb')}
    del _L0_attn_all

    def _L0_ffn_setup():
        import jax, jax.numpy as jnp
        import numpy as np
        TOP_K = 2
        key = jax.random.key(seed)
        ks = jax.random.split(key, 8)
        B, S, H, F, E = (1, 256, 256, 256, 8)
        Fs = 2 * F
        s = lambda k, shape, scale: jax.random.normal(k, shape, dtype=jnp.float32) * scale
        return {'x': s(ks[0], (B, S, H), 1.0), 'router_w': s(ks[1], (H, E), 0.02), 'gate_w': s(ks[2], (E, H, F), 0.02), 'up_w': s(ks[3], (E, H, F), 0.02), 'down_w': s(ks[4], (E, F, H), 0.02), 'shared_gate_w': s(ks[5], (H, Fs), 0.02), 'shared_up_w': s(ks[6], (H, Fs), 0.02), 'shared_down_w': s(ks[7], (Fs, H), 0.02)}
    _L0_ffn_all = _L0_ffn_setup()
    _L0_ffn_in = {k: v for k, v in _L0_ffn_all.items() if k in ('router_w', 'gate_w', 'up_w', 'down_w', 'shared_gate_w', 'shared_up_w', 'shared_down_w')}
    del _L0_ffn_all
    return {'x': x, 'L0_tok_W': _L0_tok_in['W'], 'L0_tok_b': _L0_tok_in['b'], 'L0_tok_cls_token': _L0_tok_in['cls_token'], 'L0_tok_pos_embed': _L0_tok_in['pos_embed'], 'L0_attn_Wq': _L0_attn_in['Wq'], 'L0_attn_Wkv': _L0_attn_in['Wkv'], 'L0_attn_Wout': _L0_attn_in['Wout'], 'L0_attn_b_out': _L0_attn_in['b_out'], 'L0_attn_pos_emb': _L0_attn_in['pos_emb'], 'L0_ffn_router_w': _L0_ffn_in['router_w'], 'L0_ffn_gate_w': _L0_ffn_in['gate_w'], 'L0_ffn_up_w': _L0_ffn_in['up_w'], 'L0_ffn_down_w': _L0_ffn_in['down_w'], 'L0_ffn_shared_gate_w': _L0_ffn_in['shared_gate_w'], 'L0_ffn_shared_up_w': _L0_ffn_in['shared_up_w'], 'L0_ffn_shared_down_w': _L0_ffn_in['shared_down_w']}

def reference(x, L0_tok_W, L0_tok_b, L0_tok_cls_token, L0_tok_pos_embed, L0_attn_Wq, L0_attn_Wkv, L0_attn_Wout, L0_attn_b_out, L0_attn_pos_emb, L0_ffn_router_w, L0_ffn_gate_w, L0_ffn_up_w, L0_ffn_down_w, L0_ffn_shared_gate_w, L0_ffn_shared_up_w, L0_ffn_shared_down_w):
    import jax
    import jax.numpy as jnp

    def _L0_tok_ref(x, W, b, cls_token, pos_embed):
        import jax, jax.numpy as jnp
        import numpy as np
        IMG = 96
        PATCH = 16
        C_IN = 3
        EMBED = 256
        NPH = IMG // PATCH
        NUM_PATCHES = NPH * NPH
        PATCH_DIM = PATCH * PATCH * C_IN
        B, C, H, Wd = x.shape
        nph, npw = (H // PATCH, Wd // PATCH)
        patches = x.reshape(B, C, nph, PATCH, npw, PATCH)
        patches = patches.transpose(0, 2, 4, 1, 3, 5)
        patches = patches.reshape(B, nph * npw, C * PATCH * PATCH)
        proj = jnp.einsum('bnd,ed->bne', patches, W) + b
        cls = jnp.broadcast_to(cls_token, (B, 1, cls_token.shape[-1]))
        out = jnp.concatenate([cls, proj], axis=1) + pos_embed
        return out

    def _L0_attn_ref(x, Wq, Wkv, Wout, b_out, pos_emb):
        import jax, jax.numpy as jnp
        import numpy as np
        HEADS = 16
        DIM_HEAD = 64
        T_MAX = DIM_HEAD

        def _cope(q, sim, pos_emb):
            G = jax.nn.sigmoid(sim)
            P = jnp.flip(jnp.cumsum(jnp.flip(G, axis=-1), axis=-1), axis=-1)
            P = jnp.minimum(P, T_MAX - 1)
            P_floor = jnp.floor(P)
            P_ceil_i = jnp.ceil(P).astype(jnp.int32)
            P_floor_i = P_floor.astype(jnp.int32)
            E = jnp.einsum('bnc,ct->bnt', q, pos_emb)
            E_ceil = jnp.take_along_axis(E, P_ceil_i, axis=-1)
            E_floor = jnp.take_along_axis(E, P_floor_i, axis=-1)
            w = P - P_floor
            return w * E_ceil + (1.0 - w) * E_floor
        B, N, D = x.shape
        h, d = (HEADS, DIM_HEAD)
        scale = d ** (-0.5)
        q = x @ Wq
        kv = x @ Wkv
        k, v = jnp.split(kv, 2, axis=-1)

        def to_heads(t):
            return t.reshape(B, N, h, d).transpose(0, 2, 1, 3).reshape(B * h, N, d)
        q, k, v = (to_heads(q), to_heads(k), to_heads(v))
        sim = jnp.einsum('bid,bjd->bij', q, k) * scale
        sim = sim + _cope(q, sim, pos_emb)
        attn = jax.nn.softmax(sim, axis=-1)
        out = jnp.einsum('bij,bjd->bid', attn, v)
        out = out.reshape(B, h, N, d).transpose(0, 2, 1, 3).reshape(B, N, h * d)
        return out @ Wout + b_out

    def _L0_ffn_ref(x, router_w, gate_w, up_w, down_w, shared_gate_w, shared_up_w, shared_down_w):
        import jax, jax.numpy as jnp
        import numpy as np
        TOP_K = 2
        B, S, H = x.shape
        N = B * S
        xf = x.reshape(N, H)
        scores = jax.nn.softmax(xf @ router_w, axis=-1)
        topk_scores, topk_idx = jax.lax.top_k(scores, TOP_K)
        E = scores.shape[-1]
        combine = jnp.zeros((N, E), dtype=x.dtype).at[jnp.arange(N)[:, None], topk_idx].add(topk_scores)
        g = jnp.einsum('nh,ehf->enf', xf, gate_w)
        u = jnp.einsum('nh,ehf->enf', xf, up_w)
        y = jnp.einsum('enf,efh->enh', jax.nn.silu(g) * u, down_w)
        routed = jnp.einsum('enh,ne->nh', y, combine)
        shared = jax.nn.silu(xf @ shared_gate_w) * (xf @ shared_up_w) @ shared_down_w
        return (shared + routed).reshape(B, S, H)
    h = _L0_tok_ref(x, L0_tok_W, L0_tok_b, L0_tok_cls_token, L0_tok_pos_embed)
    h = _layernorm(h + _L0_attn_ref(h, L0_attn_Wq, L0_attn_Wkv, L0_attn_Wout, L0_attn_b_out, L0_attn_pos_emb), axis=-1)
    h = _layernorm(h + _L0_ffn_ref(h, L0_ffn_router_w, L0_ffn_gate_w, L0_ffn_up_w, L0_ffn_down_w, L0_ffn_shared_gate_w, L0_ffn_shared_up_w, L0_ffn_shared_down_w), axis=-1)
    return h

_drawn_inputs = setup_inputs


def setup_inputs(seed=0):
    import zlib

    import numpy as np

    out = dict(_drawn_inputs(seed))
    spreads = {'L0_attn_b_out': (0.0, 0.1)}
    factors = {'L0_tok_b': 5.267,
     'L0_attn_Wq': 8.0,
     'L0_attn_pos_emb': 8.0,
     'L0_ffn_router_w': 8.0,
     'L0_ffn_gate_w': 8.0,
     'L0_ffn_up_w': 8.0,
     'L0_ffn_down_w': 8.0,
     'L0_ffn_shared_gate_w': 8.0,
     'L0_ffn_shared_up_w': 8.0,
     'L0_ffn_shared_down_w': 8.0}
    for name, (base, spread) in spreads.items():
        noise = np.random.default_rng([zlib.crc32(name.encode()), seed]).standard_normal(out[name].shape)
        drawn = base * np.exp(spread * noise) if base else spread * noise
        out[name] = jnp.asarray(drawn.astype(out[name].dtype))
    for name, factor in factors.items():
        out[name] = (out[name] * factor).astype(out[name].dtype)
    return out
```

```python
from contextlib import ExitStack

import concourse.bass as bass
from concourse import mybir

ALU = mybir.AluOpType
ACT = mybir.ActivationFunctionType
F32 = mybir.dt.float32
I16 = mybir.dt.int16
U32 = mybir.dt.uint32
AX_X = mybir.AxisListType.X


def vit_tower(nc, x, tok_w, tok_b, cls_token, pos_embed, wq, wkv, wout, b_out, cope_emb,
              router_w, gate_w, up_w, down_w, sh_gate_w, sh_up_w, sh_down_w, out):
    P = 128
    IMGS, CH, SIDE, _ = x.shape
    EMB, PD = tok_w.shape
    TOK = pos_embed.shape[1]
    PATCH = 16
    NPH = SIDE // PATCH
    KE = EMB // P
    KP = PD // P
    INNER = wq.shape[1]
    DH = cope_emb.shape[0]
    HEADS = INNER // DH
    FT = INNER // P
    NEXP, _, FF = gate_w.shape
    SH = sh_gate_w.shape[1] // FF
    NFF = SH + NEXP
    TPG = 3
    ROWS = TPG * TOK
    G = -(-IMGS // TPG)
    XR = TPG * CH * NPH
    NPAT = TPG * NPH * NPH
    SL = TOK + 2
    HB = HEADS // 2
    SCALE = float(DH) ** -0.5
    RNE = 12582912.0
    EPS = 1e-5
    SHIFTS = [32, 16, 8, 4, 2]
    assert TOK + 1 < 64 and FF == 256 and EMB == 256 and ROWS <= P

    with ExitStack() as ctx:
        def sb(name, shape, dt=F32):
            return ctx.enter_context(nc.sbuf_tensor(name, shape, dt))

        def sem(name):
            return ctx.enter_context(nc.semaphore(name))

        tokT = sb("tokT", [P, KP, EMB])
        wq_sb = sb("wq_sb", [P, KE, INNER])
        wkv_sb = sb("wkv_sb", [P, KE, 2 * INNER])
        wout_sb = sb("wout_sb", [P, FT, EMB])
        gu_sb = sb("gu_sb", [P, NEXP, KE, 2, FF])
        down_sb = sb("down_sb", [P, NEXP, KE, EMB])
        sgu_sb = sb("sgu_sb", [P, SH, KE, 2, FF])
        sdown_sb = sb("sdown_sb", [P, SH * KE, EMB])
        rw_sb = sb("rw_sb", [P, KE, NEXP])
        bout_b = sb("bout_b", [P, EMB])
        pe_nat = sb("pe_nat", [TOK + 2, EMB])
        posT = sb("posT", [P, KE, TOK + 2])
        cope_nat = sb("cope_nat", [P, DH])
        ident = sb("ident", [P, P])
        same_img = sb("same_img", [P, TPG, TOK])
        cope_bd = sb("cope_bd", [P, 2, SL])
        posb = sb("posb", [P, KE, TOK])
        scan_keep = sb("scan_keep", [P, HEADS, SL])
        iota8 = sb("iota8", [P, NEXP])
        neg_half = sb("neg_half", [P, 1])
        x_sb = sb("x_sb", [XR, PATCH * SIDE])
        xp_sb = sb("xp_sb", [XR, NPH, PATCH * PATCH])
        patT = sb("patT", [P, 2, NPH, XR])
        hT = sb("hT", [P, KE, TPG, TOK])
        htok = sb("htok", [P, EMB])
        qD = sb("qD", [P, FT, TPG, ROWS])
        qT = sb("qT", [P, FT, TPG, TOK])
        kBD = sb("kBD", [P, FT, TPG, 2, TOK])
        v_sb = sb("v_sb", [P, INNER])
        th = sb("th", [P, HEADS, TOK])
        simS = sb("simS", [P, HEADS, TOK])
        gate = sb("gate", [P, HEADS, SL])
        u = sb("u", [P, HEADS, SL])
        rr = sb("rr", [P, HEADS, SL])
        dI = sb("dI", [P, HEADS, SL], I16)
        dE = sb("dE", [P, HEADS, SL], I16)
        bit = sb("bit", [P, len(SHIFTS), HEADS, SL], I16)
        q = rr
        qpos = sb("qpos", [P, HEADS, TOK], I16)
        nb = sb("nb", [P, HEADS, TOK])
        lg = sb("lg", [P, HEADS, TOK])
        attn = sb("attn", [P, HEADS, TPG, TOK])
        mx = sb("mx", [P, HEADS])
        w_nat = attn[:].rearrange("p h b j -> p (h b j)")[:, :KE * PD].rearrange("p (t d) -> p t d", t=KE)
        den = sb("den", [P, HEADS])
        rden = sb("rden", [P, HEADS])
        attnT = sb("attnT", [P, HEADS, ROWS])
        up = attnT[:].rearrange("p h r -> p (h r)")[:, :HEADS * SL].rearrange("p (h a) -> p h a", a=SL)
        o_sb = sb("o_sb", [P, INNER])
        oT = sb("oT", [P, FT, ROWS])
        res1 = sb("res1", [P, EMB])
        h1 = sb("h1", [P, EMB])
        h1T = sb("h1T", [P, KE, ROWS])
        st1 = sb("st1", [P, 6])
        mv1 = sb("mv1", [P, 2])
        ve1 = sb("ve1", [P, 1])
        rs1 = sb("rs1", [P, 1])
        st2 = sb("st2", [P, 6])
        mv2 = sb("mv2", [P, 2])
        ve2 = sb("ve2", [P, 1])
        rs2 = sb("rs2", [P, 1])
        rmax = sb("rmax", [P, 1])
        rlg = sb("rlg", [P, NEXP])
        rexp = sb("rexp", [P, NEXP])
        rsum = sb("rsum", [P, 1])
        rinv = sb("rinv", [P, 1])
        rsc = sb("rsc", [P, NEXP])
        top = sb("top", [P, 8])
        topi = sb("topi", [P, 8], U32)
        topf = sb("topf", [P, 8])
        c1 = sb("c1", [P, NEXP])
        c2 = sb("c2", [P, NEXP])
        comb = sb("comb", [P, NEXP])
        thg = sb("thg", [P, 2, FF])
        sg = sb("sg", [P, 2, FF])
        hid = sb("hid", [P, 2, FF])
        hidT = sb("hidT", [P, 2, KE, ROWS])
        res2 = sb("res2", [P, EMB])
        out_sb = sb("out_sb", [P, EMB])

        ps_g = ctx.enter_context(nc.psum_tensor("ps_g", [P, 2, 512], F32))
        ps_t = ctx.enter_context(nc.psum_tensor("ps_t", [P, 2, 512], F32))
        ps_e = ctx.enter_context(nc.psum_tensor("ps_e", [P, 2, 512], F32))
        ps_s = ctx.enter_context(nc.psum_tensor("ps_s", [P, 512], F32))
        ps_acc = ctx.enter_context(nc.psum_tensor("ps_acc", [P, 512], F32))

        w_tok = sem("w_tok")
        w_q = sem("w_q")
        w_kv = sem("w_kv")
        w_o = sem("w_o")
        w_ffn = sem("w_ffn")
        w_small = sem("w_small")
        zeroed = sem("zeroed")
        consts = sem("consts")
        setup_t = sem("setup_t")
        setup_sb = sem("setup_sb")
        tables = sem("tables")
        x_in = sem("x_in")
        xp_ready = sem("xp_ready")
        qT_ready = sem("qT_ready")
        xt_done = sem("xt_done")
        xt_sb = sem("xt_sb")
        emb_done = sem("emb_done")
        hT_ready = sem("hT_ready")
        qk_done = sem("qk_done")
        qk_sb = sem("qk_sb")
        sim_done = sem("sim_done")
        tanh_sb = sem("tanh_sb")
        sim_sb = sem("sim_sb")
        cope_done = sem("cope_done")
        v_done = sem("v_done")
        v_ready = sem("v_ready")
        ht_done = sem("ht_done")
        ht_sb = sem("ht_sb")
        htok_ready = sem("htok_ready")
        logits = sem("logits")
        attn_ready = sem("attn_ready")
        at_done = sem("at_done")
        at_sb = sem("at_sb")
        o_done = sem("o_done")
        o_ready = sem("o_ready")
        ot_done = sem("ot_done")
        ot_sb = sem("ot_sb")
        proj_done = sem("proj_done")
        res1_done = sem("res1_done")
        var1 = sem("var1")
        rstd1 = sem("rstd1")
        h1_ready = sem("h1_ready")
        h1t_done = sem("h1t_done")
        h1t_sb = sem("h1t_sb")
        rout_done = sem("rout_done")
        rlg_ready = sem("rlg_ready")
        rexp_ready = sem("rexp_ready")
        gu_done = sem("gu_done")
        thg_ready = sem("thg_ready")
        hid_ready = sem("hid_ready")
        hidt_done = sem("hidt_done")
        hidt_sb = sem("hidt_sb")
        ffn_done = sem("ffn_done")
        res2_done = sem("res2_done")
        var2 = sem("var2")
        rstd2 = sem("rstd2")
        out_ready = sem("out_ready")
        stored = sem("stored")
        dve_attn = sem("dve_attn")
        dve_ffn = sem("dve_ffn")
        DVE_ATTN = 26
        DVE_FFN = 21

        def first(g):
            return isinstance(g, int) and g == 0

        x_rows = x.rearrange("b c (r i) w -> (b c r) (i w)", i=PATCH)
        out_rows = out.rearrange("b t e -> (b t) e")

        def apart(eng):
            eng.nop(nofuse=True)

        def diagonal(ap):
            dims = list(ap.ap)
            step, n = dims[-2]
            return bass.AP(ap.tensor, ap.offset, dims[:-2] + [[step + TOK, n], [dims[-1][0], TOK]])

        block = ctx.enter_context(nc.Block())

        @block.sync
        def _(sp):
            def load_x(g, row):
                if not first(g):
                    sp.wait_ge(xp_ready, g)
                sp.dma_start(x_sb[:, :], x_rows[bass.ds(row, XR), :]).then_inc(x_in, 16)

            def store(g, row, lo, hi):
                sp.wait_ge(out_ready, g + 1)
                n = (hi - lo) // 16 * 16
                sp.dma_start(out_rows[bass.ds(row, n), :], out_sb[lo:lo + n, :]).then_inc(stored, 16)
                sp.dma_start(out_rows[bass.ds(row + n, hi - lo - n), :], out_sb[lo + n:hi, :]).then_inc(stored, 16)

            sp.dma_start(w_nat[:, :, :], tok_w.rearrange("(t p) d -> p t d", p=P)).then_inc(w_tok, 16)
            load_x(0, 0)
            sp.dma_start(pe_nat[:TOK, :], pos_embed[0]).then_inc(w_small, 16)
            sp.dma_start(pe_nat[TOK:TOK + 1, :], tok_b.rearrange("(a e) -> a e", a=1)).then_inc(w_small, 16)
            sp.dma_start(pe_nat[TOK + 1:, :], cls_token[0]).then_inc(w_small, 16)
            for h in range(2):
                sp.dma_start(cope_nat[DH * h:DH * h + DH, :], cope_emb).then_inc(w_small, 16)
            sp.dma_start(wq_sb[:, :, :], wq.rearrange("(t p) n -> p t n", p=P)).then_inc(w_q, 16)
            sp.dma_start(wkv_sb[:, :, :], wkv.rearrange("(t p) n -> p t n", p=P)).then_inc(w_kv, 16)
            sp.dma_start(wout_sb[:, :, :], wout.rearrange("(t p) n -> p t n", p=P)).then_inc(w_o, 16)
            sp.dma_start(bout_b[:, :], b_out.partition_broadcast(P)).then_inc(w_o, 16)
            sp.dma_start(rw_sb[:, :, :], router_w.rearrange("(t p) e -> p t e", p=P)).then_inc(w_ffn, 16)
            for t in range(KE):
                rows = slice(P * t, P * t + P)
                for j, w in enumerate((sh_gate_w, sh_up_w)):
                    sp.dma_start(sgu_sb[:, :, t, j, :], w[rows, :].rearrange("p (s f) -> p s f", f=FF)
                                 ).then_inc(w_ffn, 16)
                for j, w in enumerate((gate_w, up_w)):
                    sp.dma_start(gu_sb[:, :, t, j, :], w[:, rows, :].rearrange("e p f -> p e f")
                                 ).then_inc(w_ffn, 16)
                sp.dma_start(down_sb[:, :, t, :], down_w[:, rows, :].rearrange("e p n -> p e n")
                             ).then_inc(w_ffn, 16)
            sp.dma_start(sdown_sb[:, :, :], sh_down_w.rearrange("(t p) n -> p t n", p=P)).then_inc(w_ffn, 16)

            load_x(1, XR)
            with sp.Fori(2, G - 1) as t:
                load_x(t, t * XR)
                store(t - 2, (t - 2) * ROWS, 0, ROWS)
            load_x(G - 1, (IMGS - TPG) * CH * NPH)
            store(G - 3, (G - 3) * ROWS, 0, ROWS)
            store(G - 2, (G - 2) * ROWS, 0, ROWS)
            done = (G - 1) * TPG
            store(G - 1, done * TOK, (done - IMGS + TPG) * TOK, ROWS)
            sp.wait_ge(stored, 32 * G + 1)

        N_W_FFN = 16 * (2 + 5 * KE)

        @block.gpsimd
        def _(pool):
            for buf in (qD, kBD, cope_bd, gate):
                nc.gpsimd.memset(buf[:], 0.0).then_inc(zeroed, 1)
            nc.gpsimd.memset(scan_keep[:], 1.0).then_inc(consts, 1)
            nc.gpsimd.memset(ident[:], 1.0).then_inc(consts, 1)
            nc.gpsimd.memset(same_img[:], 1.0).then_inc(consts, 1)
            nc.gpsimd.memset(neg_half[:], -0.5).then_inc(consts, 1)
            nc.gpsimd.iota(iota8[:], pattern=[[1, NEXP]], base=0, channel_multiplier=0,
                           allow_small_or_imprecise_dtypes=True).then_inc(consts, 1)
            pool.wait_ge(consts, 5)
            nc.gpsimd.affine_select(out=ident[:], in_=ident[:], compare_op=ALU.is_equal, fill=0.0, base=0,
                                    pattern=[[-1, P]], channel_multiplier=1).then_inc(consts, 1)
            nc.gpsimd.affine_select(out=same_img[:], in_=same_img[:], compare_op=ALU.is_ge, fill=0.0, base=0,
                                    pattern=[[-TOK, TPG], [0, TOK]], channel_multiplier=1).then_inc(consts, 1)
            nc.gpsimd.memset(scan_keep[:, :, SL - 1:SL], 0.0).then_inc(consts, 1)
            pool.wait_ge(consts, 8)
            nc.gpsimd.affine_select(out=same_img[:], in_=same_img[:], compare_op=ALU.is_ge, fill=0.0,
                                    base=TOK - 1, pattern=[[TOK, TPG], [0, TOK]],
                                    channel_multiplier=-1).then_inc(consts, 1)

            def regroup(g):
                pool.wait_ge(x_in, g * 16 + 16)
                if not first(g):
                    pool.wait_ge(xt_done, g * 2)
                apart(pool)
                nc.gpsimd.tensor_copy(xp_sb[:, :, :].rearrange("p r (i w) -> p r i w", w=PATCH),
                                      x_sb[:, :].rearrange("p (i r w) -> p r i w", r=NPH, w=PATCH)
                                      ).then_inc(xp_ready, 1)

            def stage1(g):
                for s in range(2):
                    pool.wait_ge(qk_sb, g * 4 + s + 1)
                    apart(pool)
                    for f in range(4 * s, 4 * s + 4):
                        ins = nc.gpsimd.tensor_copy(qT[:, f], diagonal(qD[:, f]))
                    ins.then_inc(qT_ready, 1)
                pool.wait_ge(ht_sb, g + 1)
                if first(g):
                    pool.wait_ge(w_o, 32)
                nc.gpsimd.tensor_tensor(htok[:ROWS], htok[:ROWS], bout_b[:ROWS], ALU.add).then_inc(htok_ready, 1)

            def norm(g, var, ve, rs, rstd):
                pool.wait_ge(var, g + 1)
                nc.gpsimd.tensor_tensor(rs[:ROWS], ve[:ROWS], neg_half[:ROWS], ALU.pow).then_inc(rstd, 1)

            regroup(0)
            stage1(0)
            regroup(1)
            norm(0, var1, ve1, rs1, rstd1)
            with pool.Fori(1, G - 1) as t:
                stage1(t)
                regroup(t + 1)
                norm(t - 1, var2, ve2, rs2, rstd2)
                norm(t, var1, ve1, rs1, rstd1)
            stage1(G - 1)
            norm(G - 2, var2, ve2, rs2, rstd2)
            norm(G - 1, var1, ve1, rs1, rstd1)
            norm(G - 1, var2, ve2, rs2, rstd2)

        @block.tensor
        def _(pe):
            def stage1(g):
                pe.wait_ge(xp_ready, g + 1)
                apart(pe)
                for half in range(2):
                    for c in range(NPH):
                        mm = nc.tensor.transpose(ps_g[:, half, c * XR:(c + 1) * XR],
                                                 xp_sb[:, c, P * half:P * half + P], ident[:XR, :XR])
                    mm.then_inc(xt_done, 1)
                pe.wait_ge(xt_sb, g * 2 + 2)
                pt = patT[:, :, :, :].rearrange("p h c (b k r) -> p h c b k r", b=TPG, k=CH)
                for m in range(KE):
                    for k in range(KP):
                        mm = nc.tensor.matmul(ps_t[:, 0, m * NPAT:(m + 1) * NPAT], tokT[:, k, m * P:(m + 1) * P],
                                              pt[:, k % 2, :, :, k // 2, :], start=(k == 0), stop=(k == KP - 1))
                mm.then_inc(emb_done, 1)
                pe.wait_ge(hT_ready, (g + 1) * KE)
                if first(g):
                    pe.wait_ge(w_q, 16)
                    pe.wait_ge(w_kv, 16)
                banks = [ps_t[:, 1], ps_g[:, 0], ps_g[:, 1], ps_t[:, 0]]
                for s, bank in enumerate(banks):
                    w = wq_sb if s < 2 else wkv_sb
                    for f in range(4):
                        c = (4 * (s % 2) + f) * P
                        for k in range(KE):
                            mm = nc.tensor.matmul(bank[:, f * ROWS:(f + 1) * ROWS], w[:, k, c:c + P],
                                                  hT[:, k], start=(k == 0), stop=(k == KE - 1))
                    mm.then_inc(qk_done, 1)
                pe.wait_ge(qk_sb, g * 4 + 4)
                for s, bank in enumerate([ps_t[:, 1], ps_g[:, 0]]):
                    for f in range(4):
                        for b in range(TPG):
                            mm = nc.tensor.matmul(bank[:ROWS, f * 2 * TOK:(f + 1) * 2 * TOK],
                                                  qD[:, 4 * s + f, b], kBD[:, 4 * s + f, b],
                                                  start=(b == 0), stop=(b == TPG - 1))
                    mm.then_inc(sim_done, 1)
                for s, bank in enumerate([ps_g[:, 1], ps_t[:, 0]]):
                    for k in range(KE):
                        mm = nc.tensor.matmul(bank[:ROWS], hT[:, k],
                                              wkv_sb[:, k, INNER + 512 * s:INNER + 512 * s + 512],
                                              start=(k == 0), stop=(k == KE - 1))
                    mm.then_inc(v_done, 1)
                pe.wait_ge(sim_sb, g * 2 + 1)
                for k in range(KE):
                    mm = nc.tensor.transpose(ps_t[:ROWS, 1, k * P:(k + 1) * P],
                                             hT[:, k].rearrange("p b t -> p (b t)"), ident[:])
                mm.then_inc(ht_done, 1)
                pe.wait_ge(qT_ready, g * 2 + 2)
                for f in range(FT):
                    c = f % 4 * 2 * SL
                    mm = nc.tensor.matmul(ps_e[:ROWS, f // 4, c:c + 2 * SL], qT[:, f], cope_bd[:, :, :],
                                          start=True, stop=True)
                mm.then_inc(cope_done, 1)

            def stage2(g):
                pe.wait_ge(attn_ready, g + 1)
                for s in range(4):
                    bank = (ps_g[:, s] if s < 2 else ps_t[:, s - 2])
                    for i in range(4):
                        mm = nc.tensor.transpose(bank[:ROWS, i * ROWS:(i + 1) * ROWS], attn[:ROWS, 4 * s + i],
                                                 ident[:ROWS, :ROWS])
                    mm.then_inc(at_done, 1)
                pe.wait_ge(v_ready, g * 2 + 2)
                for h in range(HEADS):
                    if h % 4 == 0:
                        pe.wait_ge(at_sb, g * 4 + h // 4 + 1)
                    mm = nc.tensor.matmul(ps_e[:ROWS, h // HB, h % HB * DH:h % HB * DH + DH], attnT[:ROWS, h],
                                          v_sb[:ROWS, h * DH:h * DH + DH], start=True, stop=True)
                    if h % HB == HB - 1:
                        mm.then_inc(o_done, 1)
                for s in range(2):
                    pe.wait_ge(o_ready, g * 2 + s + 1)
                    for f in range(4):
                        c = (4 * s + f) * P
                        mm = nc.tensor.transpose(ps_g[:, s, f * ROWS:(f + 1) * ROWS], o_sb[:ROWS, c:c + P],
                                                 ident[:ROWS, :ROWS])
                    mm.then_inc(ot_done, 1)
                if first(g):
                    pe.wait_ge(w_o, 32)
                for f in range(FT):
                    if f % 4 == 0:
                        pe.wait_ge(ot_sb, g * 2 + f // 4 + 1)
                    mm = nc.tensor.matmul(ps_s[:ROWS, :EMB], oT[:, f], wout_sb[:, f, :],
                                          start=(f == 0), stop=(f == FT - 1))
                mm.then_inc(proj_done, 1)

            def ffn(f, after):
                pe.wait_ge(h1_ready, f + 1)
                if after is not None:
                    pe.wait_ge(sim_sb, after * 2 + 2)
                for k in range(KE):
                    mm = nc.tensor.transpose(ps_g[:, 0, k * ROWS:(k + 1) * ROWS], h1[:ROWS, k * P:(k + 1) * P],
                                             ident[:ROWS, :ROWS])
                mm.then_inc(h1t_done, 1)
                pe.wait_ge(h1t_sb, f + 1)
                for k in range(KE):
                    mm = nc.tensor.matmul(ps_s[:ROWS, :NEXP], h1T[:, k], rw_sb[:, k, :],
                                          start=(k == 0), stop=(k == KE - 1))
                mm.then_inc(rout_done, 1)
                if after is not None:
                    pe.wait_ge(v_ready, after * 2 + 2)
                    pe.wait_ge(ht_sb, after + 1)
                pe.wait_ge(res2_done, f + 1)

                def gate_up(i):
                    w = sgu_sb[:, i] if i < SH else gu_sb[:, i - SH]
                    for k in range(KE):
                        mm = nc.tensor.matmul(ps_g[:ROWS, (i + 1) % 2], h1T[:, k], w[:, k],
                                              start=(k == 0), stop=(k == KE - 1))
                    mm.then_inc(gu_done, 1)

                gate_up(0)
                gate_up(1)
                for i in range(NFF):
                    pe.wait_ge(hid_ready, f * NFF + i + 1)
                    for k in range(KE):
                        mm = nc.tensor.transpose(ps_t[:, i % 2, k * ROWS:(k + 1) * ROWS],
                                                 hid[:ROWS, i % 2, k * P:(k + 1) * P], ident[:ROWS, :ROWS])
                    mm.then_inc(hidt_done, 1)
                    if i + 2 < NFF:
                        gate_up(i + 2)
                    pe.wait_ge(hidt_sb, f * NFF + i + 1)
                    for k in range(KE):
                        w = sdown_sb[:, i * KE + k] if i < SH else down_sb[:, i - SH, k]
                        mm = nc.tensor.matmul(ps_acc[:ROWS, :EMB], hidT[:, i % 2, k], w,
                                              start=(i == 0 and k == 0), stop=(i == NFF - 1 and k == KE - 1))
                mm.then_inc(ffn_done, 1)

            pe.wait_ge(w_tok, 16)
            pe.wait_ge(consts, 9)
            for s, bank in enumerate([ps_g[:, 0], ps_g[:, 1], ps_t[:, 0]]):
                for j in range(2):
                    for m in range(KE):
                        mm = nc.tensor.transpose(bank[:, j * EMB + m * P:j * EMB + m * P + P],
                                                 w_nat[:, m, (2 * s + j) * P:(2 * s + j + 1) * P], ident[:])
                mm.then_inc(setup_t, 1)
            pe.wait_ge(w_small, 80)
            for m in range(KE):
                mm = nc.tensor.transpose(ps_t[:, 1, m * (TOK + 2):(m + 1) * (TOK + 2)],
                                         pe_nat[:, m * P:(m + 1) * P], ident[:TOK + 2, :TOK + 2])
            mm.then_inc(setup_t, 1)
            pe.wait_ge(setup_sb, 3)
            pe.wait_ge(tables, 7)
            pe.wait_ge(zeroed, 4)

            stage1(0)
            stage2(0)
            pe.wait_ge(w_ffn, N_W_FFN)
            with pe.Fori(1, G) as t:
                stage1(t)
                ffn(t - 1, t)
                stage2(t)
            ffn(G - 1, None)

        @block.scalar
        def _(act):
            def stage1(g):
                for half in range(2):
                    act.wait_ge(xt_done, g * 2 + half + 1)
                    nc.scalar.copy(patT[:, half], ps_g[:, half, :NPH * XR].rearrange("p (c n) -> p c n", n=XR)
                                   ).then_inc(xt_sb, 1)
                banks = [ps_t[:, 1], ps_g[:, 0], ps_g[:, 1], ps_t[:, 0]]
                for s, bank in enumerate(banks):
                    act.wait_ge(qk_done, g * 4 + s + 1)
                    src = bank[:, :4 * ROWS].rearrange("p (f b t) -> p f b t", f=4, b=TPG)
                    if s < 2:
                        nc.scalar.copy(diagonal(qD[:, 4 * s:4 * s + 4]), src).then_inc(qk_sb, 1)
                    else:
                        dst = kBD[:, 4 * (s - 2):4 * (s - 2) + 4]
                        nc.scalar.copy(dst[:DH, :, :, 0], src[:DH])
                        nc.scalar.copy(dst[DH:, :, :, 1], src[DH:]).then_inc(qk_sb, 1)
                for s, bank in enumerate([ps_t[:, 1], ps_g[:, 0]]):
                    act.wait_ge(sim_done, g * 2 + s + 1)
                    src = bank[:ROWS, :HB * TOK].rearrange("p (h j) -> p h j", j=TOK)
                    nc.scalar.activation(th[:ROWS, HB * s:HB * s + HB], src, ACT.Tanh, scale=0.5 * SCALE
                                         ).then_inc(tanh_sb, 1)
                    nc.scalar.mul(simS[:ROWS, HB * s:HB * s + HB], src, SCALE).then_inc(sim_sb, 1)
                for s, bank in enumerate([ps_g[:, 1], ps_t[:, 0]]):
                    act.wait_ge(v_done, g * 2 + s + 1)
                    nc.scalar.copy(v_sb[:ROWS, 512 * s:512 * s + 512], bank[:ROWS]).then_inc(v_ready, 1)
                act.wait_ge(ht_done, g + 1)
                if not first(g):
                    act.wait_ge(res1_done, g)
                nc.scalar.copy(htok[:ROWS], ps_t[:ROWS, 1, :EMB]).then_inc(ht_sb, 1)

            def stage2(g):
                for s in range(2):
                    act.wait_ge(ot_done, g * 2 + s + 1)
                    nc.scalar.copy(oT[:, 4 * s:4 * s + 4],
                                   ps_g[:, s, :4 * ROWS].rearrange("p (f r) -> p f r", f=4)).then_inc(ot_sb, 1)

            def softmax_exp(g):
                act.wait_ge(logits, g + 1)
                nc.scalar.activation(attn[:ROWS], lg[:ROWS].unsqueeze(2).to_broadcast([ROWS, HEADS, TPG, TOK]),
                                     ACT.Exp).then_inc(attn_ready, 1)

            def ffn(f, g):
                act.wait_ge(h1t_done, f + 1)
                nc.scalar.copy(h1T[:], ps_g[:, 0, :KE * ROWS].rearrange("p (k r) -> p k r", k=KE)
                               ).then_inc(h1t_sb, 1)

                def gate_tanh(i):
                    act.wait_ge(gu_done, f * NFF + i + 1)
                    nc.scalar.activation(thg[:ROWS, i % 2], ps_g[:ROWS, (i + 1) % 2, :FF], ACT.Tanh, scale=0.5
                                         ).then_inc(thg_ready, 1)

                gate_tanh(0)
                act.wait_ge(rlg_ready, f + 1)
                nc.scalar.activation(rexp[:ROWS], rlg[:ROWS], ACT.Exp, accum_out=rsum[:ROWS]
                                     ).then_inc(rexp_ready, 1)
                gate_tanh(1)
                for i in range(NFF):
                    act.wait_ge(hidt_done, f * NFF + i + 1)
                    nc.scalar.copy(hidT[:, i % 2], ps_t[:, i % 2, :KE * ROWS].rearrange("p (k r) -> p k r", k=KE)
                                   ).then_inc(hidt_sb, 1)
                    if i + 2 < NFF:
                        gate_tanh(i + 2)
                    if i == NFF - 1 and g is not None:
                        softmax_exp(g)

            act.wait_ge(setup_t, 3)
            for s, bank in enumerate([ps_g[:, 0], ps_g[:, 1], ps_t[:, 0]]):
                nc.scalar.copy(tokT[:, 2 * s:2 * s + 2], bank.rearrange("p (j e) -> p j e", j=2)
                               ).then_inc(setup_sb, 1)
            act.wait_ge(zeroed, 4)
            stage1(0)
            softmax_exp(0)
            stage2(0)
            with act.Fori(1, G) as t:
                stage1(t)
                ffn(t - 1, t)
                stage2(t)
            ffn(G - 1, None)

        @block.vector
        def _(dve):
            class Steps:

                def __init__(self, sem, per):
                    self.sem, self.per, self.n = sem, per, 0

                def did(self, ins):
                    ins.then_inc(self.sem, 1)
                    self.n += 1

                def settle(self, g):
                    dve.wait_ge(self.sem, g * self.per + self.n)

                def end(self):
                    assert self.n == self.per, (self.n, self.per)
                    self.n = 0

            A = Steps(dve_attn, DVE_ATTN)
            F = Steps(dve_ffn, DVE_FFN)
            V = nc.vector

            def embed(g):
                dve.wait_ge(emb_done, g + 1)
                for m in range(KE):
                    src = ps_t[:, 0, m * NPAT:(m + 1) * NPAT].rearrange("p (c b r) -> p c b r", c=NPH, b=TPG)
                    dst = hT[:, m, :, 1:].rearrange("p b (r c) -> p c b r", c=NPH)
                    pos = posb[:, m, 1:].rearrange("p (r c) -> p c r", c=NPH).unsqueeze(2).to_broadcast(
                        [P, NPH, TPG, NPH])
                    V.tensor_tensor(dst, src, pos, ALU.add).then_inc(hT_ready, 1)

            table = ps_e[:ROWS, :, :HB * SL].rearrange("p s (h a) -> p s h a", a=SL)

            def split(t, a0, a1):
                return t[:ROWS, :, a0:a1].rearrange("p (s h) a -> p s h a", s=2)

            def flat(t):
                return t[:ROWS].rearrange("p h a -> p (h a)")

            def cope(g, part):
                if part == 0:
                    dve.wait_ge(tanh_sb, g * 2 + 2)
                    A.did(V.tensor_scalar(gate[:ROWS, :, 1:1 + TOK], th[:ROWS], -0.5, 0.5, ALU.mult, ALU.add))
                if part == 1:
                    A.settle(g)
                    A.did(V.tensor_tensor_scan(flat(u)[:, ::-1], flat(scan_keep)[:, ::-1], flat(gate)[:, ::-1],
                                               0.0, ALU.mult, ALU.add))
                if part == 2:
                    A.settle(g)
                    A.did(V.tensor_scalar(flat(rr), flat(u), RNE, -RNE, ALU.add, ALU.add))
                    A.settle(g)
                    A.did(V.tensor_tensor(flat(up), flat(u), flat(rr), ALU.is_gt))
                    A.settle(g)
                    A.did(V.tensor_tensor(flat(dI), flat(rr), flat(up), ALU.add))
                if part == 3:
                    A.settle(g)
                    A.did(V.tensor_scalar(flat(dE), flat(dI), 62, None, ALU.bitwise_and))
                    for n, d in enumerate(SHIFTS):
                        ins = V.tensor_scalar(bit[:ROWS, n].rearrange("p h a -> p (h a)"), flat(dI), d, None,
                                              ALU.bitwise_and)
                    A.did(ins)
                    A.settle(g)
                    A.did(V.tensor_tensor(flat(q), flat(u), flat(dE), ALU.subtract))
                if part == 4:
                    dve.wait_ge(cope_done, g + 1)
                    for n, d in enumerate(SHIFTS):
                        A.settle(g)
                        apart(dve)
                        A.did(V.copy_predicated(table[:, :, :, 0:SL - d], split(bit[:, n], 0, SL - d),
                                                table[:, :, :, d:SL]))
                if part == 5:
                    A.settle(g)
                    A.did(V.tensor_scalar(qpos[:ROWS], q[:ROWS, :, 1:1 + TOK], 0.0, None, ALU.is_gt))
                    A.did(V.tensor_copy(split(nb, 0, TOK), table[:, :, :, 0:TOK]))
                    A.settle(g)
                    apart(dve)
                    A.did(V.copy_predicated(split(nb, 0, TOK), split(qpos, 0, TOK), table[:, :, :, 2:2 + TOK]))
                    A.did(V.tensor_scalar(flat(q).bitcast(U32), flat(q).bitcast(U32), 0x7FFFFFFF, None,
                                          ALU.bitwise_and))
                if part == 6:
                    centre = table[:, :, :, 1:1 + TOK]
                    A.settle(g)
                    A.did(V.tensor_tensor(split(nb, 0, TOK), split(nb, 0, TOK), centre, ALU.subtract))
                    A.settle(g)
                    A.did(V.tensor_tensor(nb[:ROWS], q[:ROWS, :, 1:1 + TOK], nb[:ROWS], ALU.mult))
                    A.settle(g)
                    A.did(V.tensor_tensor(split(nb, 0, TOK), split(nb, 0, TOK), centre, ALU.add))
                if part == 7:
                    dve.wait_ge(sim_sb, g * 2 + 2)
                    A.settle(g)
                    A.did(V.tensor_tensor(nb[:ROWS], nb[:ROWS], simS[:ROWS], ALU.add))
                    A.settle(g)
                    A.did(V.tensor_reduce(mx[:ROWS], nb[:ROWS], AX_X, ALU.max))
                    A.settle(g)
                    V.tensor_tensor(lg[:ROWS], nb[:ROWS], mx[:ROWS].unsqueeze(2).to_broadcast([ROWS, HEADS, TOK]),
                                    ALU.subtract).then_inc(logits, 1)

            def attention(g):
                dve.wait_ge(attn_ready, g + 1)
                A.did(V.tensor_reduce(den[:ROWS], attn[:ROWS, :, 0], AX_X, ALU.add))
                A.settle(g)
                A.did(V.reciprocal(rden[:ROWS], den[:ROWS]))
                keep = same_img[:ROWS].rearrange("p b j -> p (b j)").unsqueeze(1).to_broadcast([ROWS, 4, ROWS])
                for s in range(4):
                    bank = (ps_g[:, s] if s < 2 else ps_t[:, s - 2])
                    dve.wait_ge(at_done, g * 4 + s + 1)
                    V.tensor_tensor(attnT[:ROWS, 4 * s:4 * s + 4],
                                    bank[:ROWS, :4 * ROWS].rearrange("p (h r) -> p h r", h=4), keep, ALU.mult
                                    ).then_inc(at_sb, 1)
                A.settle(g)
                for s in range(2):
                    dve.wait_ge(o_done, g * 2 + s + 1)
                    scale = rden[:ROWS, HB * s:HB * s + HB].unsqueeze(2).to_broadcast([ROWS, HB, DH])
                    V.tensor_tensor(o_sb[:ROWS, 512 * s:512 * s + 512].rearrange("p (h d) -> p h d", d=DH),
                                    ps_e[:ROWS, s].rearrange("p (h d) -> p h d", d=DH), scale, ALU.mult
                                    ).then_inc(o_ready, 1)

            def norm1(g):
                dve.wait_ge(proj_done, g + 1)
                dve.wait_ge(htok_ready, g + 1)
                V.tensor_tensor(res1[:ROWS], ps_s[:ROWS, :EMB], htok[:ROWS], ALU.add).then_inc(res1_done, 1)
                dve.wait_ge(res1_done, g + 1)
                A.did(V.bn_stats(st1[:ROWS], res1[:ROWS]))
                A.settle(g)
                apart(dve)
                A.did(V.bn_aggr(mv1[:ROWS], st1[:ROWS]))
                A.settle(g)
                V.tensor_scalar(ve1[:ROWS], mv1[:ROWS, 1:2], EPS, None, ALU.add).then_inc(var1, 1)
                dve.wait_ge(rstd1, g + 1)
                V.tensor_scalar(h1[:ROWS], res1[:ROWS], mv1[:ROWS, 0:1], rs1[:ROWS], ALU.subtract, ALU.mult
                                ).then_inc(h1_ready, 1)
                A.end()

            def router(f, part):
                if part == 0:
                    dve.wait_ge(rout_done, f + 1)
                    F.did(V.tensor_reduce(rmax[:ROWS], ps_s[:ROWS, :NEXP], AX_X, ALU.max))
                    F.settle(f)
                    V.tensor_scalar(rlg[:ROWS], ps_s[:ROWS, :NEXP], rmax[:ROWS], None, ALU.subtract
                                    ).then_inc(rlg_ready, 1)
                if part == 1:
                    dve.wait_ge(rexp_ready, f + 1)
                    F.did(V.reciprocal(rinv[:ROWS], rsum[:ROWS]))
                    F.settle(f)
                    F.did(V.tensor_scalar(rsc[:ROWS], rexp[:ROWS], rinv[:ROWS], 0.5, ALU.mult, ALU.mult))
                    F.settle(f)
                    apart(dve)
                    F.did(V.max(top[:ROWS], rsc[:ROWS]))
                    F.settle(f)
                    apart(dve)
                    F.did(V.max_index(topi[:ROWS], top[:ROWS], rsc[:ROWS]))
                    F.settle(f)
                    F.did(V.tensor_copy(topf[:ROWS], topi[:ROWS]))
                    F.settle(f)
                    F.did(V.tensor_scalar(c1[:ROWS], iota8[:ROWS], topf[:ROWS, 0:1], top[:ROWS, 0:1],
                                          ALU.is_equal, ALU.mult))
                    F.did(V.tensor_scalar(c2[:ROWS], iota8[:ROWS], topf[:ROWS, 1:2], top[:ROWS, 1:2],
                                          ALU.is_equal, ALU.mult))
                    F.settle(f)
                    F.did(V.tensor_tensor(comb[:ROWS], c1[:ROWS], c2[:ROWS], ALU.add))
                    F.settle(f)

            def hidden(f, i):
                bank = ps_g[:ROWS, (i + 1) % 2]
                dve.wait_ge(thg_ready, f * NFF + i + 1)
                F.did(V.scalar_tensor_tensor(sg[:ROWS, i % 2], thg[:ROWS, i % 2], 1.0, bank[:, :FF],
                                             ALU.add, ALU.mult))
                F.settle(f)
                weight = 0.5 if i < SH else comb[:ROWS, i - SH:i - SH + 1]
                V.scalar_tensor_tensor(hid[:ROWS, i % 2], sg[:ROWS, i % 2], weight, bank[:, FF:],
                                       ALU.mult, ALU.mult).then_inc(hid_ready, 1)

            def norm2(f):
                dve.wait_ge(ffn_done, f + 1)
                V.tensor_tensor(res2[:ROWS], ps_acc[:ROWS, :EMB], h1[:ROWS], ALU.add).then_inc(res2_done, 1)
                dve.wait_ge(res2_done, f + 2)
                F.did(V.bn_stats(st2[:ROWS], res2[:ROWS]))
                F.settle(f)
                apart(dve)
                F.did(V.bn_aggr(mv2[:ROWS], st2[:ROWS]))
                F.settle(f)
                V.tensor_scalar(ve2[:ROWS], mv2[:ROWS, 1:2], EPS, None, ALU.add).then_inc(var2, 1)
                dve.wait_ge(rstd2, f + 1)
                dve.wait_ge(stored, 32 * f + 1)
                V.tensor_scalar(out_sb[:ROWS], res2[:ROWS], mv2[:ROWS, 0:1], rs2[:ROWS], ALU.subtract, ALU.mult
                                ).then_inc(out_ready, 1)
                F.end()

            def ffn(f, g):
                router(f, 0)
                hidden(f, 0)
                router(f, 1)
                for i in range(1, NFF):
                    hidden(f, i)
                    if g is not None and i <= 8:
                        cope(g, i - 1)

            dve.wait_ge(setup_t, 4)
            dve.wait_ge(zeroed, 4)
            V.tensor_copy(posT[:], ps_t[:, 1, :KE * (TOK + 2)].rearrange("p (m t) -> p m t", m=KE)
                          ).then_inc(tables, 1)
            dve.wait_ge(tables, 1)
            for m in range(KE):
                V.tensor_scalar(posb[:, m, 1:], posT[:, m, 1:TOK], posT[:, m, TOK:TOK + 1], None, ALU.add
                                ).then_inc(tables, 1)
                V.tensor_tensor(hT[:, m, :, 0:1], posT[:, m, 0:1].unsqueeze(1).to_broadcast([P, TPG, 1]),
                                posT[:, m, TOK + 1:].unsqueeze(1).to_broadcast([P, TPG, 1]), ALU.add
                                ).then_inc(tables, 1)
            for h in range(2):
                part = slice(DH * h, DH * h + DH)
                V.tensor_copy(cope_bd[part, h, :], cope_nat[part, SL - 1::-1]).then_inc(tables, 1)
            V.memset(res2[:], 0.0).then_inc(res2_done, 1)
            V.memset(out_sb[:], 0.0).then_inc(stored, 1)
            dve.wait_ge(consts, 9)
            dve.wait_ge(tables, 7)

            embed(0)
            for part in range(8):
                cope(0, part)
            attention(0)
            norm1(0)
            with dve.Fori(1, G) as t:
                embed(t)
                ffn(t - 1, t)
                norm2(t - 1)
                attention(t)
                norm1(t)
            ffn(G - 1, None)
            norm2(G - 1)


_INS = ['x', 'L0_tok_W', 'L0_tok_b', 'L0_tok_cls_token', 'L0_tok_pos_embed', 'L0_attn_Wq', 'L0_attn_Wkv',
        'L0_attn_Wout', 'L0_attn_b_out', 'L0_attn_pos_emb', 'L0_ffn_router_w', 'L0_ffn_gate_w', 'L0_ffn_up_w',
        'L0_ffn_down_w', 'L0_ffn_shared_gate_w', 'L0_ffn_shared_up_w', 'L0_ffn_shared_down_w']
_OUTS = [((64, 37, 256), 'float32')]


def kernel(**inputs):
    import numpy as _np
    import concourse.bacc as _bacc
    from concourse import mybir as _mybir
    from concourse.bass_utils import run_bass_kernel_spmd as _run

    nc = _bacc.Bacc("TRN2", target_bir_lowering=False, num_devices=1)
    arrays, args = {}, []
    for name in _INS:
        a = _np.ascontiguousarray(inputs[name])
        arrays[f"in_{name}_dram"] = a
        args.append(nc.dram_tensor(f"in_{name}_dram", a.shape, _mybir.dt.from_np(a.dtype), kind="ExternalInput").ap())
    for i, (shape, dtype) in enumerate(_OUTS):
        dt = _mybir.dt.from_np(_np.dtype(dtype))
        args.append(nc.dram_tensor(f"out_{i}_dram", shape, dt, kind="ExternalOutput").ap())
    vit_tower(nc, *args)
    r = _run(nc, [arrays], core_ids=[0])
    got = tuple(r.results[0][f"out_{i}_dram"] for i in range(len(_OUTS)))
    return got[0]
```

```python
from contextlib import ExitStack

import concourse.bass as bass
from concourse import mybir

ALU = mybir.AluOpType
ACT = mybir.ActivationFunctionType
F32 = mybir.dt.float32
I16 = mybir.dt.int16
I32 = mybir.dt.int32
U32 = mybir.dt.uint32
AX_X = mybir.AxisListType.X


def vit_tower(nc, x, tok_w, tok_b, cls_token, pos_embed, wq, wkv, wout, b_out, cope_emb,
              router_w, gate_w, up_w, down_w, sh_gate_w, sh_up_w, sh_down_w, out):
    P = 128
    IMGS, CH, SIDE, _ = x.shape
    EMB, PD = tok_w.shape
    TOK = pos_embed.shape[1]
    PATCH = 16
    NPH = SIDE // PATCH
    KE = EMB // P
    KP = PD // P
    INNER = wq.shape[1]
    DH = cope_emb.shape[0]
    HEADS = INNER // DH
    FT = INNER // P
    NEXP, _, FF = gate_w.shape
    SH = sh_gate_w.shape[1] // FF
    TOPK = 2
    TPG = 3
    ROWS = TPG * TOK
    G = -(-IMGS // TPG)
    XR = TPG * CH * NPH
    NPAT = TPG * NPH * NPH
    SL = TOK + 2
    SLP = 48
    HB = HEADS // 2
    SCALE = float(DH) ** -0.5
    RNE = 12582912.0
    EPS = 1e-5
    SHIFTS = [32, 16, 8, 4, 2]
    REC = EMB + TOPK
    TOKENS = G * ROWS
    CAP = -(-G * ROWS // P) * P
    NT = (TOPK * G * ROWS - NEXP) // P + NEXP
    SLOTS = NEXP * CAP + NT * P
    assert NT % 4 == 2 and SLOTS % P == 0 and G % 4 == 2
    assert TOK + 1 < 64 and FF == 256 and EMB == 256 and ROWS <= P

    with ExitStack() as ctx:
        def sb(name, shape, dt=F32):
            return ctx.enter_context(nc.sbuf_tensor(name, shape, dt))

        def sem(name):
            return ctx.enter_context(nc.semaphore(name))

        tokT = sb("tokT", [P, KP, EMB])
        wq_sb = sb("wq_sb", [P, KE, INNER])
        wkv_sb = sb("wkv_sb", [P, KE, 2 * INNER])
        wout_sb = sb("wout_sb", [P, FT, EMB])
        gu_sb = sb("gu_sb", [P, NEXP, KE, 2, FF])
        down_sb = sb("down_sb", [P, NEXP, KE, EMB])
        sgu_sb = sb("sgu_sb", [P, SH, KE, 2, FF])
        sdown_sb = sb("sdown_sb", [P, SH * KE, EMB])
        rw_sb = sb("rw_sb", [P, KE, NEXP])
        bout_b = sb("bout_b", [P, EMB])
        pe_nat = sb("pe_nat", [TOK + 2, EMB])
        posT = sb("posT", [P, KE, TOK + 2])
        cope_nat = sb("cope_nat", [P, DH])
        ident = sb("ident", [P, P])
        same_img = sb("same_img", [P, TPG, TOK])
        own_img = sb("own_img", [P, TPG], I16)
        cope_bd = sb("cope_bd", [P, 2, SLP])
        posb = sb("posb", [P, KE, TOK])
        scan_keep = sb("scan_keep", [P, HEADS, SL])
        iota8 = sb("iota8", [P, NEXP])
        neg_half = sb("neg_half", [P, 1])
        x_sb = sb("x_sb", [XR, PATCH * SIDE])
        xp_sb = sb("xp_sb", [XR, NPH, PATCH * PATCH])
        patT = sb("patT", [P, 2, NPH, XR])
        hT = sb("hT", [P, KE, TPG, TOK])
        htok = sb("htok", [P, EMB])
        qT = sb("qT", [P, FT, ROWS])
        qBD = sb("qBD", [P, FT, 2, ROWS])
        kT = sb("kT", [P, FT, ROWS])
        v_sb = sb("v_sb", [P, INNER])
        th = sb("th", [P, HEADS, TOK])
        simS = sb("simS", [P, HEADS, TOK])
        gate = sb("gate", [P, HEADS, SL])
        u = sb("u", [P, HEADS, SL])
        rr = sb("rr", [P, HEADS, SL])
        dI = sb("dI", [P, HEADS, SL], I16)
        dE = sb("dE", [P, HEADS, SL], I16)
        bit = sb("bit", [P, len(SHIFTS), HEADS, SL], I16)
        q = rr
        qpos = sb("qpos", [P, HEADS, TOK], I16)
        nb = sb("nb", [P, HEADS, TOK])
        lg = sb("lg", [P, HEADS, TOK])
        ex = sb("ex", [P, HEADS, TOK])
        attn = sb("attn", [P, HEADS, TPG, TOK])
        mx = sb("mx", [P, HEADS])
        w_nat = attn[:].rearrange("p h b j -> p (h b j)")[:, :KE * PD].rearrange("p (t d) -> p t d", t=KE)
        den = sb("den", [P, HEADS])
        rden = sb("rden", [P, HEADS])
        attnT = sb("attnT", [P, HEADS, ROWS])
        up = sb("up", [P, HEADS, SL])
        oT = sb("oT", [P, FT, ROWS])
        res1 = sb("res1", [P, EMB])
        h1 = sb("h1", [P, EMB])
        h1T = sb("h1T", [P, KE, ROWS])
        st1 = sb("st1", [P, 6])
        mv1 = sb("mv1", [P, 2])
        ve1 = sb("ve1", [P, 1])
        rs1 = sb("rs1", [P, 1])
        rmax = sb("rmax", [P, 1])
        rlg = sb("rlg", [P, NEXP])
        rexp = sb("rexp", [P, NEXP])
        rsum = sb("rsum", [P, 1])
        rinv = sb("rinv", [P, 1])
        rsc = sb("rsc", [P, NEXP])
        top = sb("top", [P, 8])
        topi = sb("topi", [P, 8], U32)
        topf = sb("topf", [P, 8])
        c1 = sb("c1", [P, NEXP])
        c2 = sb("c2", [P, NEXP])
        chosen = sb("chosen", [P, NEXP])
        earlier = sb("earlier", [P, NEXP])
        slot8 = sb("slot8", [P, NEXP])
        pick = sb("pick", [P, TOPK, NEXP])
        slotf = sb("slotf", [P, TOPK])
        idf = sb("idf", [P, 1])
        ids = sb("ids", [P, TOPK], U32)
        rec = sb("rec", [P, REC])
        slotu = sb("slotu", [P, TOPK], U32)
        thg = sb("thg", [P, 2, FF])
        sg = sb("sg", [P, 2, FF])
        hid = sb("hid", [P, 2, FF])
        hidT = sb("hidT", [P, 2, KE, P])
        earlier_than = sb("earlier_than", [P, P])
        ones = sb("ones", [P, P])
        slot0 = sb("slot0", [P, NEXP])
        no_ids = sb("no_ids", [P, SLOTS // P], U32)
        tile_no = sb("tile_no", [P, NT])
        past = sb("past", [P, NT, NEXP])
        cnt = sb("cnt", [P, 3, NEXP])
        tl = sb("tl", [P, 3, NT])
        tile_expert = sb("tile_expert", [P, NT], I32)
        tile_slot = sb("tile_slot", [P, NT], I32)
        ids_in = sb("ids_in", [P, 4], U32)
        ids_t = sb("ids_t", [P, 4], U32)
        ids_y = sb("ids_y", [P, 4], U32)
        spare = attnT[:].rearrange("p h r -> p (h r)")
        xgT = spare[:, :4 * P].rearrange("p (i k r) -> p i k r", i=2, k=KE)
        y_sb = spare[:, 4 * P:4 * P + 2 * EMB].rearrange("p (i e) -> p i e", i=2)
        xg = attn[:].rearrange("p h b j -> p (h b j)")[:, :4 * EMB].rearrange("p (b e) -> p b e", b=4)
        NB = 4
        last_a = wkv_sb[:].rearrange("p k n -> p (k n)")
        yc = last_a[:, :2 * NB * EMB].rearrange("p (b j e) -> p b j e", b=NB, j=TOPK)
        resc = last_a[:, 2 * NB * EMB:3 * NB * EMB].rearrange("p (b e) -> p b e", b=NB)
        outc = last_a[:, 3 * NB * EMB:].rearrange("p (b e) -> p b e", b=NB)
        recc = wq_sb[:].rearrange("p k n -> p (k n)")[:, :NB * REC].rearrange("p (b e) -> p b e", b=NB)
        stc = sb("stc", [P, NB, 6])
        mvc = sb("mvc", [P, NB, 2])
        vec = sb("vec", [P, G])
        rsc2 = sb("rsc2", [P, G])

        h1_d = nc.dram_tensor("h1_d", [TOPK * TOKENS, EMB], F32, kind="Internal").ap()
        rec_d = nc.dram_tensor("rec_d", [TOKENS, REC], F32, kind="Internal").ap()
        ids_d = nc.dram_tensor("ids_d", [SLOTS, 1], U32, kind="Internal").ap()
        y_d = nc.dram_tensor("y_d", [TOPK * TOKENS, EMB], F32, kind="Internal").ap()

        ps_g = ctx.enter_context(nc.psum_tensor("ps_g", [P, 2, 512], F32))
        ps_t = ctx.enter_context(nc.psum_tensor("ps_t", [P, 2, 512], F32))
        ps_e = ctx.enter_context(nc.psum_tensor("ps_e", [P, 2, 512], F32))
        ps_s = ctx.enter_context(nc.psum_tensor("ps_s", [P, 512], F32))
        ps_acc = ctx.enter_context(nc.psum_tensor("ps_acc", [P, 512], F32))

        w_tok = sem("w_tok")
        w_q = sem("w_q")
        w_kv = sem("w_kv")
        w_o = sem("w_o")
        w_ffn = sem("w_ffn")
        w_small = sem("w_small")
        zeroed = sem("zeroed")
        consts = sem("consts")
        setup_t = sem("setup_t")
        setup_sb = sem("setup_sb")
        tables = sem("tables")
        x_in = sem("x_in")
        xp_ready = sem("xp_ready")
        xt_done = sem("xt_done")
        xt_sb = sem("xt_sb")
        emb_done = sem("emb_done")
        hT_ready = sem("hT_ready")
        qk_done = sem("qk_done")
        qk_sb = sem("qk_sb")
        sim_done = sem("sim_done")
        tanh_sb = sem("tanh_sb")
        sim_first = sem("sim_first")
        sim_sb = sem("sim_sb")
        cope_done = sem("cope_done")
        v_done = sem("v_done")
        v_ready = sem("v_ready")
        ht_done = sem("ht_done")
        ht_sb = sem("ht_sb")
        htok_ready = sem("htok_ready")
        logits = sem("logits")
        exp_ready = sem("exp_ready")
        weights = sem("weights")
        attn_ready = sem("attn_ready")
        at_done = sem("at_done")
        at_sb = sem("at_sb")
        o_done = sem("o_done")
        ot_sb = sem("ot_sb")
        proj_done = sem("proj_done")
        res1_done = sem("res1_done")
        var1 = sem("var1")
        rstd1 = sem("rstd1")
        h1_ready = sem("h1_ready")
        h1t_done = sem("h1t_done")
        h1t_sb = sem("h1t_sb")
        rout_done = sem("rout_done")
        rlg_ready = sem("rlg_ready")
        rexp_ready = sem("rexp_ready")
        gu_done = sem("gu_done")
        thg_ready = sem("thg_ready")
        hid_ready = sem("hid_ready")
        hidt_done = sem("hidt_done")
        hidt_sb = sem("hidt_sb")
        ffn_done = sem("ffn_done")
        chosen_ready = sem("chosen_ready")
        rank_done = sem("rank_done")
        sum_read = sem("sum_read")
        rec_ready = sem("rec_ready")
        h1_stored = sem("h1_stored")
        rec_stored = sem("rec_stored")
        ids_stored = sem("ids_stored")
        ids_left = sem("ids_left")
        ids_zeroed = sem("ids_zeroed")
        counted = sem("counted")
        tiles_ready = sem("tiles_ready")
        ids_taken = sem("ids_taken")
        ids_kept = sem("ids_kept")
        xg_zeroed = sem("xg_zeroed")
        tile_ids = [sem(f"tile_ids_{i}") for i in range(4)]
        tile_x = [sem(f"tile_x_{i}") for i in range(4)]
        tile_xt = sem("tile_xt")
        tile_xt_sb = sem("tile_xt_sb")
        tile_gu = sem("tile_gu")
        tile_tanh = sem("tile_tanh")
        tile_hid = sem("tile_hid")
        tile_hidt = sem("tile_hidt")
        tile_hidt_sb = sem("tile_hidt_sb")
        tile_y = sem("tile_y")
        tile_y_sb = sem("tile_y_sb")
        tile_stored = [sem(f"tile_stored_{i}") for i in range(4)]
        rec_in = [sem(f"rec_in_{i}") for i in range(NB)]
        res2_done = sem("res2_done")
        var2 = sem("var2")
        rstd2 = sem("rstd2")
        out_ready = sem("out_ready")
        stored = [sem(f"stored_{i}") for i in range(NB)]
        dve_tab = sem("dve_tab")
        dve_tile = sem("dve_tile")
        dve_last = sem("dve_last")
        dve_attn = sem("dve_attn")
        dve_soft = sem("dve_soft")
        dve_ffn = sem("dve_ffn")
        DVE_ATTN = 24
        DVE_SOFT = 4
        DVE_FFN = 19

        NFF = SH

        N_CONSTS = 17

        def first(g):
            return isinstance(g, int) and g == 0

        x_rows = x.rearrange("b c (r i) w -> (b c r) (i w)", i=PATCH)
        out_rows = out.rearrange("b t e -> (b t) e")

        def split(t, a0, a1):
            return t[:ROWS, :, a0:a1].rearrange("p (k h) a -> p k h a", h=4)

        def halves(t, a0, a1):
            return t[:ROWS, :, a0:a1].rearrange("p (k h) a -> p k h a", h=HB)

        def apart(eng):
            eng.nop(nofuse=True)

        block = ctx.enter_context(nc.Block())

        @block.sync
        def _(sp):
            def load_x(g, row):
                if not first(g):
                    sp.wait_ge(xp_ready, g)
                sp.dma_start(x_sb[:, :], x_rows[bass.ds(row, XR), :]).then_inc(x_in, 16)

            def store_rows(g, row):
                sp.wait_ge(h1_ready, g + 1)
                for j in range(TOPK):
                    sp.dma_start(h1_d[bass.ds(row + j * TOKENS, ROWS), :], h1[:ROWS]).then_inc(h1_stored, 16)
                sp.wait_ge(rec_ready, g + 1)
                sp.dma_start(rec_d[bass.ds(row, ROWS), :], rec[:ROWS]).then_inc(rec_stored, 16)

            sp.dma_start(w_nat[:, :, :], tok_w.rearrange("(t p) d -> p t d", p=P)).then_inc(w_tok, 16)
            load_x(0, 0)
            sp.dma_start(pe_nat[:TOK, :], pos_embed[0]).then_inc(w_small, 16)
            sp.dma_start(pe_nat[TOK:TOK + 1, :], tok_b.rearrange("(a e) -> a e", a=1)).then_inc(w_small, 16)
            sp.dma_start(pe_nat[TOK + 1:, :], cls_token[0]).then_inc(w_small, 16)
            for h in range(2):
                sp.dma_start(cope_nat[DH * h:DH * h + DH, :], cope_emb).then_inc(w_small, 16)
            sp.dma_start(wq_sb[:, :, :], wq.rearrange("(t p) n -> p t n", p=P)).then_inc(w_q, 16)
            sp.dma_start(wkv_sb[:, :, :], wkv.rearrange("(t p) n -> p t n", p=P)).then_inc(w_kv, 16)
            sp.dma_start(wout_sb[:, :, :], wout.rearrange("(t p) n -> p t n", p=P)).then_inc(w_o, 16)
            sp.dma_start(bout_b[:, :], b_out.partition_broadcast(P)).then_inc(w_o, 16)
            sp.dma_start(rw_sb[:, :, :], router_w.rearrange("(t p) e -> p t e", p=P)).then_inc(w_ffn, 16)
            for t in range(KE):
                rows = slice(P * t, P * t + P)
                for j, w in enumerate((sh_gate_w, sh_up_w)):
                    sp.dma_start(sgu_sb[:, :, t, j, :], w[rows, :].rearrange("p (s f) -> p s f", f=FF)
                                 ).then_inc(w_ffn, 16)
                for j, w in enumerate((gate_w, up_w)):
                    sp.dma_start(gu_sb[:, :, t, j, :], w[:, rows, :].rearrange("e p f -> p e f")
                                 ).then_inc(w_ffn, 16)
                sp.dma_start(down_sb[:, :, t, :], down_w[:, rows, :].rearrange("e p n -> p e n")
                             ).then_inc(w_ffn, 16)
            sp.dma_start(sdown_sb[:, :, :], sh_down_w.rearrange("(t p) n -> p t n", p=P)).then_inc(w_ffn, 16)

            sp.wait_ge(consts, N_CONSTS)
            sp.dma_start(ids_d.rearrange("(p n) o -> p (n o)", p=P), no_ids[:, :]).then_inc(ids_zeroed, 16)
            load_x(1, XR)
            with sp.Fori(2, G - 1) as t:
                load_x(t, t * XR)
                store_rows(t - 2, (t - 2) * ROWS)
            load_x(G - 1, (IMGS - TPG) * CH * NPH)
            for g in range(G - 3, G):
                store_rows(g, g * ROWS)

            def load_ids(t, b):
                slot = nc.sync.value_load(tile_slot[0:1, bass.ds(t, 1)], min_val=0, max_val=SLOTS - P)
                sp.dma_start(ids_in[:, b:b + 1], ids_d[bass.ds(slot, P), :]).then_inc(tile_ids[b], 16)

            sp.wait_ge(tiles_ready, 1)
            sp.wait_ge(ids_stored, 16 * TOPK * G)
            for t in range(4):
                load_ids(t, t)
            with sp.Fori(0, NT // 4 - 1) as four:
                for b in range(4):
                    t = four * 4 + b
                    sp.wait_ge(ids_taken, t + 1)
                    load_ids(t + 4, b)
            for t in range(NT - 6, NT - 4):
                sp.wait_ge(ids_taken, t + 1)
                load_ids(t + 4, t % 4)

            def load_rec(g, row, b):
                sp.dma_start(recc[:ROWS, b], rec_d[bass.ds(row, ROWS), :]).then_inc(rec_in[b], 16)
                for j in range(TOPK):
                    sp.dma_start(yc[:ROWS, b, j], y_d[bass.ds(row + j * TOKENS, ROWS), :]).then_inc(rec_in[b], 16)

            def store(g, row, b, lo):
                sp.wait_ge(out_ready, g + 1)
                n = (ROWS - lo) // 16 * 16
                sp.dma_start(out_rows[bass.ds(row, n), :], outc[lo:lo + n, b]).then_inc(stored[b], 16)
                sp.dma_start(out_rows[bass.ds(row + n, ROWS - lo - n), :], outc[lo + n:ROWS, b]
                             ).then_inc(stored[b], 16)

            sp.wait_ge(rec_stored, 16 * G + 1)
            for b in range(4):
                sp.wait_ge(tile_stored[b], 16 * -(-(NT - b) // 4))
            for g in range(NB):
                load_rec(g, g * ROWS, g)
            with sp.Fori(0, (G - 2) // NB - 1) as four:
                for b in range(NB):
                    g = four * NB + b
                    store(g, g * ROWS, b, 0)
                    load_rec(g + NB, (g + NB) * ROWS, b)
            for g in range(G - 2 - NB, G):
                if g < G - 1:
                    store(g, g * ROWS, g % NB, 0)
                if g + NB < G:
                    load_rec(g + NB, (g + NB) * ROWS, g % NB)
            done = (G - 1) * TPG
            store(G - 1, done * TOK, (G - 1) % NB, (done - IMGS + TPG) * TOK)
            for b in range(NB):
                sp.wait_ge(stored[b], 32 * -(-(G - b) // NB))
            sp.wait_ge(h1_stored, 16 * TOPK * G)

        N_W_FFN = 16 * (2 + 5 * KE)

        @block.gpsimd
        def _(pool):
            for buf in (qBD, cope_bd, gate):
                nc.gpsimd.memset(buf[:], 0.0).then_inc(zeroed, 1)
            nc.gpsimd.memset(scan_keep[:], 1.0).then_inc(consts, 1)
            nc.gpsimd.memset(ident[:], 1.0).then_inc(consts, 1)
            nc.gpsimd.memset(same_img[:], 1.0).then_inc(consts, 1)
            nc.gpsimd.memset(neg_half[:], -0.5).then_inc(consts, 1)
            nc.gpsimd.iota(iota8[:], pattern=[[1, NEXP]], base=0, channel_multiplier=0,
                           allow_small_or_imprecise_dtypes=True).then_inc(consts, 1)
            nc.gpsimd.memset(ones[:], 1.0).then_inc(consts, 1)
            nc.gpsimd.memset(earlier_than[:], 1.0).then_inc(consts, 1)
            nc.gpsimd.memset(earlier[:], 0.0).then_inc(consts, 1)
            nc.gpsimd.memset(no_ids[:], TOPK * TOKENS).then_inc(consts, 1)
            for table, pattern, row in ((slot0, [[CAP, NEXP]], 0), (tile_no, [[1, NT]], 0), (idf, [[0, 1]], 1)):
                nc.gpsimd.iota(table[:], pattern=pattern, base=0, channel_multiplier=row,
                               allow_small_or_imprecise_dtypes=True).then_inc(consts, 1)
            pool.wait_ge(consts, 12)
            nc.gpsimd.affine_select(out=ident[:], in_=ident[:], compare_op=ALU.is_equal, fill=0.0, base=0,
                                    pattern=[[-1, P]], channel_multiplier=1).then_inc(consts, 1)
            nc.gpsimd.affine_select(out=same_img[:], in_=same_img[:], compare_op=ALU.is_ge, fill=0.0, base=0,
                                    pattern=[[-TOK, TPG], [0, TOK]], channel_multiplier=1).then_inc(consts, 1)
            nc.gpsimd.memset(scan_keep[:, :, SL - 1:SL], 0.0).then_inc(consts, 1)
            nc.gpsimd.affine_select(out=earlier_than[:], in_=earlier_than[:], compare_op=ALU.is_gt, fill=0.0, base=0,
                                    pattern=[[1, P]], channel_multiplier=-1).then_inc(consts, 1)
            pool.wait_ge(consts, 16)
            nc.gpsimd.affine_select(out=same_img[:], in_=same_img[:], compare_op=ALU.is_ge, fill=0.0,
                                    base=TOK - 1, pattern=[[TOK, TPG], [0, TOK]],
                                    channel_multiplier=-1).then_inc(consts, 1)

            def regroup(g):
                pool.wait_ge(x_in, g * 16 + 16)
                if not first(g):
                    pool.wait_ge(xt_done, g * 2)
                apart(pool)
                nc.gpsimd.tensor_copy(xp_sb[:, :, :].rearrange("p r (i w) -> p r i w", w=PATCH),
                                      x_sb[:, :].rearrange("p (i r w) -> p r i w", r=NPH, w=PATCH)
                                      ).then_inc(xp_ready, 1)

            def stage1(g):
                pool.wait_ge(ht_sb, g + 1)
                if first(g):
                    pool.wait_ge(w_o, 32)
                nc.gpsimd.tensor_tensor(htok[:ROWS], htok[:ROWS], bout_b[:ROWS], ALU.add).then_inc(htok_ready, 1)

            def norm(g, var, ve, rs, rstd):
                pool.wait_ge(var, g + 1)
                nc.gpsimd.tensor_tensor(rs[:ROWS], ve[:ROWS], neg_half[:ROWS], ALU.pow).then_inc(rstd, 1)

            def scatter(f):
                pool.wait_ge(rec_ready, f + 1)
                apart(pool)
                for j in range(TOPK):
                    nc.gpsimd.indirect_dma_start(
                        ids_d[:, :], bass.IndirectOffsetOnAxis(ap=slotu[:ROWS, j:j + 1], axis=0),
                        ids[:ROWS, j:j + 1], None).then_inc(ids_stored, 16)

            def numbers_left(f):
                if not first(f):
                    pool.wait_ge(ids_stored, f * 16 * TOPK)
                apart(pool)
                pool.nop().then_inc(ids_left, 1)

            regroup(0)
            stage1(0)
            regroup(1)
            pool.wait_ge(ids_zeroed, 16)

            def middle(t):
                if not isinstance(t, int) or t < G - 1:
                    regroup(t + 1)
                norm(t - 1, var1, ve1, rs1, rstd1)
                stage1(t)
                numbers_left(t - 1)
                scatter(t - 1)

            middle(1)
            with pool.Fori(2, G - 1) as t:
                middle(t)
            middle(G - 1)
            norm(G - 1, var1, ve1, rs1, rstd1)
            numbers_left(G - 1)
            scatter(G - 1)

            LAST_ID = TOPK * TOKENS - 1

            def gather_x(t, turn, b):
                pool.wait_ge(tile_ids[b], turn * 16 + 16)
                apart(pool)
                nc.gpsimd.tensor_copy(ids_t[:, b:b + 1], ids_in[:, b:b + 1]).then_inc(ids_taken, 1)
                pool.wait_ge(ids_taken, t + 1)
                apart(pool)
                nc.gpsimd.indirect_dma_start(xg[:, b], None, h1_d[:, :],
                                             bass.IndirectOffsetOnAxis(ap=ids_t[:, b:b + 1], axis=0),
                                             bounds_check=LAST_ID, oob_is_err=False).then_inc(tile_x[b], 16)

            def keep_ids(t, turn, b):
                pool.wait_ge(tile_x[b], turn * 16 + 16)
                if not first(turn):
                    pool.wait_ge(tile_stored[b], turn * 16)
                apart(pool)
                nc.gpsimd.tensor_copy(ids_y[:, b:b + 1], ids_t[:, b:b + 1]).then_inc(ids_kept, 1)
                pool.wait_ge(ids_kept, t + 1)

            def scatter_y(t, b):
                pool.wait_ge(tile_y_sb, t + 1)
                apart(pool)
                nc.gpsimd.indirect_dma_start(y_d[:, :], bass.IndirectOffsetOnAxis(ap=ids_y[:, b:b + 1], axis=0),
                                             y_sb[:, b % 2], None, bounds_check=LAST_ID, oob_is_err=False
                                             ).then_inc(tile_stored[b], 16)

            pool.wait_ge(h1_stored, 16 * TOPK * G)
            nc.gpsimd.memset(xg[:], 0.0).then_inc(xg_zeroed, 1)
            pool.wait_ge(xg_zeroed, 1)
            def ahead(t, turn, b):
                keep_ids(t, turn, b)
                pool.wait_ge(tile_xt, t + 1)
                gather_x(t + 4, turn + 1, b)

            for t in range(4):
                gather_x(t, 0, t)
            for t in range(2):
                ahead(t, 0, t)
            for t in range(4):
                ahead(t + 2, (t + 2) // 4, (t + 2) % 4)
                scatter_y(t, t)
            with pool.Fori(1, NT // 4 - 1) as four:
                for b in range(4):
                    ahead(four * 4 + b + 2, four + (b + 2) // 4, (b + 2) % 4)
                    scatter_y(four * 4 + b, b)
            for t in range(NT - 6, NT):
                if t + 2 < NT:
                    keep_ids(t + 2, (t + 2) // 4, (t + 2) % 4)
                scatter_y(t, t % 4)

            def norm_last(g):
                pool.wait_ge(var2, g + 1)
                nc.gpsimd.tensor_tensor(rsc2[:ROWS, bass.ds(g, 1)], vec[:ROWS, bass.ds(g, 1)], neg_half[:ROWS], ALU.pow
                                        ).then_inc(rstd2, 1)

            with pool.Fori(0, G) as t:
                norm_last(t)

        @block.tensor
        def _(pe):
            def embed(g):
                if not isinstance(g, int) or g > 1:
                    pe.wait_ge(res1_done, g - 1)
                    pe.wait_ge(sum_read, g - 1)
                pe.wait_ge(xp_ready, g + 1)
                apart(pe)
                for half, bank in enumerate([ps_s, ps_acc]):
                    for c in range(NPH):
                        mm = nc.tensor.transpose(bank[:, c * XR:(c + 1) * XR],
                                                 xp_sb[:, c, P * half:P * half + P], ident[:XR, :XR])
                    mm.then_inc(xt_done, 1)
                pe.wait_ge(xt_sb, g * 2 + 2)
                pt = patT[:, :, :, :].rearrange("p h c (b k r) -> p h c b k r", b=TPG, k=CH)
                for m in range(KE):
                    for k in range(KP):
                        mm = nc.tensor.matmul(ps_t[:, 0, m * NPAT:(m + 1) * NPAT], tokT[:, k, m * P:(m + 1) * P],
                                              pt[:, k % 2, :, :, k // 2, :], start=(k == 0), stop=(k == KP - 1))
                mm.then_inc(emb_done, 1)

            def qk(g, s):
                if s == 0:
                    pe.wait_ge(hT_ready, (g + 1) * KE)
                    if not first(g):
                        pe.wait_ge(ht_sb, g)
                        pe.wait_ge(v_ready, g * 2)
                    else:
                        pe.wait_ge(w_q, 16)
                        pe.wait_ge(w_kv, 16)
                bank = [ps_t[:, 1], ps_g[:, 0], ps_g[:, 1], ps_t[:, 0]][s]
                w = wq_sb if s < 2 else wkv_sb
                for f in range(4):
                    c = (4 * (s % 2) + f) * P
                    for k in range(KE):
                        mm = nc.tensor.matmul(bank[:, f * ROWS:(f + 1) * ROWS], w[:, k, c:c + P],
                                              hT[:, k], start=(k == 0), stop=(k == KE - 1))
                mm.then_inc(qk_done, 1)

            def score(g):
                pe.wait_ge(qk_sb, g * 4 + 4)
                for s, banks in enumerate([ps_g, ps_t]):
                    for i in range(HB):
                        h = HB * s + i
                        mm = nc.tensor.matmul(banks[:ROWS, i // 4, i % 4 * ROWS:(i % 4 + 1) * ROWS],
                                              qBD[:, h // 2, h % 2], kT[:, h // 2], start=True, stop=True)
                    mm.then_inc(sim_done, 1)

            def cope_and_v(g):
                for f in range(FT):
                    c = f % 4 * 2 * SLP
                    mm = nc.tensor.matmul(ps_e[:ROWS, f // 4, c:c + 2 * SLP], qT[:, f], cope_bd[:, :, :],
                                          start=True, stop=True)
                mm.then_inc(cope_done, 1)
                for s, bank in enumerate([ps_g[:, 0], ps_g[:, 1]]):
                    for k in range(KE):
                        mm = nc.tensor.matmul(bank[:ROWS], hT[:, k],
                                              wkv_sb[:, k, INNER + 512 * s:INNER + 512 * s + 512],
                                              start=(k == 0), stop=(k == KE - 1))
                    mm.then_inc(v_done, 1)
                for k in range(KE):
                    mm = nc.tensor.transpose(ps_t[:ROWS, 1, k * P:(k + 1) * P],
                                             hT[:, k].rearrange("p b t -> p (b t)"), ident[:])
                mm.then_inc(ht_done, 1)

            def attend(g, ahead):
                if ahead is not None:
                    pe.wait_ge(sim_sb, ahead * 2 + 2)
                pe.wait_ge(attn_ready, g + 1)
                for s in range(4):
                    bank = (ps_g[:, s] if s < 2 else ps_t[:, s - 2])
                    for i in range(4):
                        mm = nc.tensor.transpose(bank[:ROWS, i * ROWS:(i + 1) * ROWS], attn[:ROWS, 4 * s + i],
                                                 ident[:ROWS, :ROWS])
                    mm.then_inc(at_done, 1)
                pe.wait_ge(v_ready, g * 2 + 2)
                for odd in range(2):
                    for h in range(odd, HEADS, 2):
                        if odd == 0 and h % 4 == 0:
                            pe.wait_ge(at_sb, g * 4 + h // 4 + 1)
                        f = h // 2
                        mm = nc.tensor.matmul(ps_e[odd * DH:odd * DH + DH, f // 4, f % 4 * ROWS:(f % 4 + 1) * ROWS],
                                              v_sb[:ROWS, h * DH:h * DH + DH], attnT[:ROWS, h],
                                              start=True, stop=True)
                        if odd and f % 4 == 3:
                            mm.then_inc(o_done, 1)
                if first(g):
                    pe.wait_ge(w_o, 32)
                for f in range(FT):
                    if f % 4 == 0:
                        pe.wait_ge(ot_sb, g * 2 + f // 4 + 1)
                    mm = nc.tensor.matmul(ps_s[:ROWS, :EMB], oT[:, f], wout_sb[:, f, :],
                                          start=(f == 0), stop=(f == FT - 1))
                mm.then_inc(proj_done, 1)

            def ffn(f, after, ahead):
                pe.wait_ge(h1_ready, f + 1)
                pe.wait_ge(v_ready, after * 2 + 2)
                for k in range(KE):
                    mm = nc.tensor.transpose(ps_g[:, 0, k * ROWS:(k + 1) * ROWS], h1[:ROWS, k * P:(k + 1) * P],
                                             ident[:ROWS, :ROWS])
                mm.then_inc(h1t_done, 1)
                pe.wait_ge(h1t_sb, f + 1)
                for k in range(KE):
                    mm = nc.tensor.matmul(ps_s[:ROWS, :NEXP], h1T[:, k], rw_sb[:, k, :],
                                          start=(k == 0), stop=(k == KE - 1))
                mm.then_inc(rout_done, 1)
                pe.wait_ge(ht_sb, after + 1)

                def gate_up(i):
                    for k in range(KE):
                        mm = nc.tensor.matmul(ps_g[:ROWS, (i + 1) % 2], h1T[:, k], sgu_sb[:, i, k],
                                              start=(k == 0), stop=(k == KE - 1))
                    mm.then_inc(gu_done, 1)

                gate_up(0)
                gate_up(1)
                if ahead is not None:
                    qk(ahead, 0)
                for i in range(NFF):
                    pe.wait_ge(hid_ready, f * NFF + i + 1)
                    for k in range(KE):
                        mm = nc.tensor.transpose([ps_t[:, 0], ps_s][i][:, k * ROWS:(k + 1) * ROWS],
                                                 hid[:ROWS, i % 2, k * P:(k + 1) * P], ident[:ROWS, :ROWS])
                    mm.then_inc(hidt_done, 1)
                    if ahead is not None and i == NFF - 1:
                        qk(ahead, 1)
                for i in range(NFF):
                    pe.wait_ge(hidt_sb, f * NFF + i + 1)
                    if i == 0:
                        pe.wait_ge(sum_read, f + 1)
                    for k in range(KE):
                        mm = nc.tensor.matmul(ps_acc[:ROWS, :EMB], hidT[:, i % 2, k, :ROWS], sdown_sb[:, i * KE + k],
                                              start=(i == 0 and k == 0), stop=(i == NFF - 1 and k == KE - 1))
                mm.then_inc(ffn_done, 1)
                if ahead is not None:
                    qk(ahead, 2)
                    qk(ahead, 3)
                pe.wait_ge(chosen_ready, f + 1)
                nc.tensor.matmul(ps_s[:ROWS, EMB:EMB + NEXP], earlier_than[:ROWS, :ROWS], chosen[:ROWS],
                                 start=True, stop=False)
                nc.tensor.matmul(ps_s[:ROWS, EMB:EMB + NEXP], ones[:ROWS, :ROWS], earlier[:ROWS],
                                 start=False, stop=True).then_inc(rank_done, 1)

            pe.wait_ge(w_tok, 16)
            pe.wait_ge(consts, N_CONSTS)
            for s, bank in enumerate([ps_g[:, 0], ps_g[:, 1], ps_t[:, 0]]):
                for j in range(2):
                    for m in range(KE):
                        mm = nc.tensor.transpose(bank[:, j * EMB + m * P:j * EMB + m * P + P],
                                                 w_nat[:, m, (2 * s + j) * P:(2 * s + j + 1) * P], ident[:])
                mm.then_inc(setup_t, 1)
            pe.wait_ge(w_small, 80)
            for m in range(KE):
                mm = nc.tensor.transpose(ps_t[:, 1, m * (TOK + 2):(m + 1) * (TOK + 2)],
                                         pe_nat[:, m * P:(m + 1) * P], ident[:TOK + 2, :TOK + 2])
            mm.then_inc(setup_t, 1)
            pe.wait_ge(setup_sb, 3)
            pe.wait_ge(tables, 8)
            pe.wait_ge(zeroed, 3)

            embed(0)
            for part in range(4):
                qk(0, part)
            score(0)
            pe.wait_ge(sim_sb, 2)
            cope_and_v(0)
            embed(1)
            pe.wait_ge(w_ffn, N_W_FFN)
            for part in range(4):
                qk(1, part)
            score(1)
            attend(0, 1)
            cope_and_v(1)
            embed(2)
            with pe.Fori(2, G - 1) as t:
                ffn(t - 2, t - 1, t)
                score(t)
                attend(t - 1, t)
                cope_and_v(t)
                embed(t + 1)
            ffn(G - 3, G - 2, G - 1)
            score(G - 1)
            attend(G - 2, G - 1)
            cope_and_v(G - 1)
            ffn(G - 2, G - 1, None)
            attend(G - 1, None)
            ffn(G - 1, G - 1, None)

            pe.wait_ge(rec_ready, G)
            nc.tensor.matmul(ps_s[:, EMB:EMB + NEXP], ones[:ROWS, :], earlier[:ROWS], start=True, stop=True
                             ).then_inc(counted, 1)

            x_banks = [ps_s, ps_acc]

            def transpose_x(t, turn, b):
                pe.wait_ge(tile_x[b], turn * 16 + 16)
                for k in range(KE):
                    mm = nc.tensor.transpose(x_banks[b % 2][:, k * P:(k + 1) * P], xg[:, b, k * P:(k + 1) * P],
                                             ident[:])
                mm.then_inc(tile_xt, 1)

            def expert(t):
                return nc.tensor.value_load(tile_expert[0:1, bass.ds(t, 1)], min_val=0, max_val=NEXP - 1)

            def gate_up_tile(t, i, e):
                pe.wait_ge(tile_xt_sb, t + 1)
                for k in range(KE):
                    mm = nc.tensor.matmul(ps_g[:, i], xgT[:, i, k],
                                          gu_sb[:, bass.ds(e, 1), k].rearrange("p o j f -> p (o j f)"),
                                          start=(k == 0), stop=(k == KE - 1))
                mm.then_inc(tile_gu, 1)

            def tile(turn, b, ahead, e, e_ahead):
                t, i = turn * 4 + b, b % 2
                pe.wait_ge(tile_hid, t + 1)
                for k in range(KE):
                    mm = nc.tensor.transpose(ps_t[:, i, k * P:(k + 1) * P], hid[:, i, k * P:(k + 1) * P], ident[:])
                mm.then_inc(tile_hidt, 1)
                if ahead >= 3:
                    transpose_x(t + 3, turn + (b + 3) // 4, (b + 3) % 4)
                if ahead >= 2:
                    gate_up_tile(t + 2, i, e_ahead)
                pe.wait_ge(tile_hidt_sb, t + 1)
                for k in range(KE):
                    mm = nc.tensor.matmul(ps_e[:, i, :EMB], hidT[:, i, k],
                                          down_sb[:, bass.ds(e, 1), k].rearrange("p o f -> p (o f)"),
                                          start=(k == 0), stop=(k == KE - 1))
                mm.then_inc(tile_y, 1)

            pe.wait_ge(tiles_ready, 1)
            transpose_x(0, 0, 0)
            transpose_x(1, 0, 1)
            gate_up_tile(0, 0, expert(0))
            transpose_x(2, 0, 2)
            gate_up_tile(1, 1, expert(1))
            with pe.Fori(0, NT // 4 - 1) as four:
                of = [expert(four * 4 + b) for b in range(6)]
                for b in range(4):
                    tile(four, b, 3, of[b], of[b + 2])
            of = [expert(t) for t in range(NT - 6, NT)] + [None, None]
            for n in range(6):
                t = NT - 6 + n
                tile(t // 4, t % 4, min(3, NT - 1 - t), of[n], of[n + 2])

        @block.scalar
        def _(act):
            def embed(g):
                for half, bank in enumerate([ps_s, ps_acc]):
                    act.wait_ge(xt_done, g * 2 + half + 1)
                    nc.scalar.copy(patT[:, half], bank[:, :NPH * XR].rearrange("p (c n) -> p c n", n=XR)
                                   ).then_inc(xt_sb, 1)

            def qk(g, s):
                bank = [ps_t[:, 1], ps_g[:, 0], ps_g[:, 1], ps_t[:, 0]][s]
                act.wait_ge(qk_done, g * 4 + s + 1)
                src = bank[:, :4 * ROWS].rearrange("p (f r) -> p f r", f=4)
                if s < 2:
                    fs = slice(4 * s, 4 * s + 4)
                    nc.scalar.copy(qBD[:DH, fs, 0], src[:DH])
                    nc.scalar.copy(qBD[DH:, fs, 1], src[DH:])
                    nc.scalar.copy(qT[:, fs], src).then_inc(qk_sb, 1)
                else:
                    nc.scalar.copy(kT[:, 4 * (s - 2):4 * (s - 2) + 4], src).then_inc(qk_sb, 1)

            def score(g):
                for s, banks in enumerate([ps_g, ps_t]):
                    act.wait_ge(sim_done, g * 2 + s + 1)
                    if not first(g):
                        act.wait_ge(logits, g)
                    nc.scalar.copy(split(simS, 0, TOK)[:, 2 * s:2 * s + 2],
                                   banks[:ROWS, :, :4 * ROWS].rearrange("p k (h r) -> p k h r", h=4)[:, :, :, :TOK]
                                   ).then_inc(sim_first, 1)

            def score_tanh(g):
                act.wait_ge(sim_sb, g * 2 + 2)
                nc.scalar.activation(th[:ROWS], simS[:ROWS], ACT.Tanh, scale=0.5 * SCALE).then_inc(tanh_sb, 1)

            def v_and_h(g):
                for s, bank in enumerate([ps_g[:, 0], ps_g[:, 1]]):
                    act.wait_ge(v_done, g * 2 + s + 1)
                    nc.scalar.copy(v_sb[:ROWS, 512 * s:512 * s + 512], bank[:ROWS]).then_inc(v_ready, 1)
                act.wait_ge(ht_done, g + 1)
                if not first(g):
                    act.wait_ge(res1_done, g)
                nc.scalar.copy(htok[:ROWS], ps_t[:ROWS, 1, :EMB]).then_inc(ht_sb, 1)

            def attend(g):
                for s in range(2):
                    act.wait_ge(o_done, g * 2 + s + 1)
                    nc.scalar.copy(oT[:, 4 * s:4 * s + 4],
                                   ps_e[:, s, :4 * ROWS].rearrange("p (f r) -> p f r", f=4)).then_inc(ot_sb, 1)

            def softmax_exp(g):
                act.wait_ge(logits, g + 1)
                nc.scalar.activation(ex[:ROWS], lg[:ROWS], ACT.Exp).then_inc(exp_ready, 1)

            def spread(g):
                act.wait_ge(weights, g + 1)
                nc.scalar.copy(attn[:ROWS], lg[:ROWS].unsqueeze(2).to_broadcast([ROWS, HEADS, TPG, TOK])
                               ).then_inc(attn_ready, 1)

            def ffn(f, ahead):
                act.wait_ge(h1t_done, f + 1)
                nc.scalar.copy(h1T[:], ps_g[:, 0, :KE * ROWS].rearrange("p (k r) -> p k r", k=KE)
                               ).then_inc(h1t_sb, 1)

                def gate_tanh(i):
                    act.wait_ge(gu_done, f * NFF + i + 1)
                    nc.scalar.activation(thg[:ROWS, i % 2], ps_g[:ROWS, (i + 1) % 2, :FF], ACT.Tanh, scale=0.5
                                         ).then_inc(thg_ready, 1)

                gate_tanh(0)
                act.wait_ge(rlg_ready, f + 1)
                nc.scalar.activation(rexp[:ROWS], rlg[:ROWS], ACT.Exp, accum_out=rsum[:ROWS]
                                     ).then_inc(rexp_ready, 1)
                gate_tanh(1)
                if ahead is not None:
                    qk(ahead, 0)
                for i in range(NFF):
                    act.wait_ge(hidt_done, f * NFF + i + 1)
                    nc.scalar.copy(hidT[:, i % 2, :, :ROWS],
                                   [ps_t[:, 0], ps_s][i][:, :KE * ROWS].rearrange("p (k r) -> p k r", k=KE)
                                   ).then_inc(hidt_sb, 1)
                if ahead is not None:
                    for part in range(1, 4):
                        qk(ahead, part)

            act.wait_ge(setup_t, 3)
            for s, bank in enumerate([ps_g[:, 0], ps_g[:, 1], ps_t[:, 0]]):
                nc.scalar.copy(tokT[:, 2 * s:2 * s + 2], bank.rearrange("p (j e) -> p j e", j=2)
                               ).then_inc(setup_sb, 1)
            act.wait_ge(zeroed, 3)
            def middle(t):
                softmax_exp(t - 1)
                score(t)
                spread(t - 1)
                score_tanh(t)
                attend(t - 1)
                v_and_h(t)

            embed(0)
            for part in range(4):
                qk(0, part)
            score(0)
            score_tanh(0)
            v_and_h(0)
            embed(1)
            for part in range(4):
                qk(1, part)
            middle(1)
            embed(2)
            with act.Fori(2, G - 1) as t:
                ffn(t - 2, t)
                middle(t)
                embed(t + 1)
            ffn(G - 3, G - 1)
            middle(G - 1)
            ffn(G - 2, None)
            softmax_exp(G - 1)
            spread(G - 1)
            attend(G - 1)
            ffn(G - 1, None)

            x_banks = [ps_s, ps_acc]

            def x_in_sbuf(t, i):
                act.wait_ge(tile_xt, t + 1)
                nc.scalar.copy(xgT[:, i], x_banks[i][:, :EMB].rearrange("p (k r) -> p k r", k=KE)
                               ).then_inc(tile_xt_sb, 1)

            def tanh_tile(t, i):
                act.wait_ge(tile_gu, t + 1)
                nc.scalar.activation(thg[:, i], ps_g[:, i, :FF], ACT.Tanh, scale=0.5).then_inc(tile_tanh, 1)

            def tile(t, i, ahead):
                act.wait_ge(tile_hidt, t + 1)
                nc.scalar.copy(hidT[:, i], ps_t[:, i, :EMB].rearrange("p (k r) -> p k r", k=KE)
                               ).then_inc(tile_hidt_sb, 1)
                if ahead >= 3:
                    x_in_sbuf(t + 3, 1 - i)
                if ahead >= 2:
                    tanh_tile(t + 2, i)

            x_in_sbuf(0, 0)
            x_in_sbuf(1, 1)
            tanh_tile(0, 0)
            act.wait_ge(tile_gu, 1)
            x_in_sbuf(2, 0)
            tanh_tile(1, 1)
            with act.Fori(0, NT // 2 - 2) as pair:
                for i in range(2):
                    tile(pair * 2 + i, i, 3)
            for t in range(NT - 4, NT):
                tile(t, t % 2, min(3, NT - 1 - t))

        @block.vector
        def _(dve):
            class Steps:

                def __init__(self, sem, per):
                    self.sem, self.per, self.n = sem, per, 0

                def did(self, ins):
                    ins.then_inc(self.sem, 1)
                    self.n += 1

                def settle(self, g):
                    dve.wait_ge(self.sem, g * self.per + self.n)

                def end(self):
                    assert self.n == self.per, (self.n, self.per)
                    self.n = 0

            A = Steps(dve_attn, DVE_ATTN)
            S = Steps(dve_soft, DVE_SOFT)
            F = Steps(dve_ffn, DVE_FFN)
            V = nc.vector

            def embed(g):
                dve.wait_ge(emb_done, g + 1)
                for m in range(KE):
                    src = ps_t[:, 0, m * NPAT:(m + 1) * NPAT].rearrange("p (c b r) -> p c b r", c=NPH, b=TPG)
                    dst = hT[:, m, :, 1:].rearrange("p b (r c) -> p c b r", c=NPH)
                    pos = posb[:, m, 1:].rearrange("p (r c) -> p c r", c=NPH).unsqueeze(2).to_broadcast(
                        [P, NPH, TPG, NPH])
                    V.tensor_tensor(dst, src, pos, ALU.add).then_inc(hT_ready, 1)

            table = ps_e[:ROWS, :, :HB * SLP].rearrange("p s (h a) -> p s h a", a=SLP)

            def flat(t):
                return t[:ROWS].rearrange("p h a -> p (h a)")

            def scores(g):
                for s, banks in enumerate([ps_g, ps_t]):
                    dve.wait_ge(sim_first, g * 2 + s + 1)
                    src = banks[:ROWS, :, :4 * ROWS].rearrange("p k (h r) -> p k h r", h=4)
                    dst = split(simS, 0, TOK)[:, 2 * s:2 * s + 2]
                    for b in range(1, TPG):
                        apart(dve)
                        own = own_img[:ROWS, b:b + 1].unsqueeze(2).unsqueeze(3).to_broadcast([ROWS, 2, 4, TOK])
                        ins = V.copy_predicated(dst, own, src[:, :, :, b * TOK:(b + 1) * TOK])
                        if b < TPG - 1:
                            A.did(ins)
                            A.settle(g)
                        else:
                            ins.then_inc(sim_sb, 1)

            def cope(g, part):
                if part == 0:
                    dve.wait_ge(tanh_sb, g + 1)
                    A.did(V.tensor_scalar(gate[:ROWS, :, 1:1 + TOK], th[:ROWS], -0.5, 0.5, ALU.mult, ALU.add))
                if part == 1:
                    A.settle(g)
                    A.did(V.tensor_tensor_scan(flat(u)[:, ::-1], flat(scan_keep)[:, ::-1], flat(gate)[:, ::-1],
                                               0.0, ALU.mult, ALU.add))
                if part == 2:
                    A.settle(g)
                    A.did(V.tensor_scalar(flat(rr), flat(u), RNE, -RNE, ALU.add, ALU.add))
                    A.settle(g)
                    A.did(V.tensor_tensor(flat(up), flat(u), flat(rr), ALU.is_gt))
                    A.settle(g)
                    A.did(V.tensor_tensor(flat(dI), flat(rr), flat(up), ALU.add))
                if part == 3:
                    A.settle(g)
                    A.did(V.tensor_scalar(flat(dE), flat(dI), 62, None, ALU.bitwise_and))
                    for n, d in enumerate(SHIFTS):
                        ins = V.tensor_scalar(bit[:ROWS, n].rearrange("p h a -> p (h a)"), flat(dI), d, None,
                                              ALU.bitwise_and)
                    A.did(ins)
                    A.settle(g)
                    A.did(V.tensor_tensor(flat(q), flat(u), flat(dE), ALU.subtract))
                if part == 4:
                    dve.wait_ge(cope_done, g + 1)
                    for n, d in enumerate(SHIFTS):
                        A.settle(g)
                        apart(dve)
                        A.did(V.copy_predicated(table[:, :, :, 0:SL - d], halves(bit[:, n], 0, SL - d),
                                                table[:, :, :, d:SL]))
                if part == 5:
                    A.settle(g)
                    A.did(V.tensor_scalar(qpos[:ROWS], q[:ROWS, :, 1:1 + TOK], 0.0, None, ALU.is_gt))
                    A.did(V.tensor_copy(halves(nb, 0, TOK), table[:, :, :, 0:TOK]))
                    A.settle(g)
                    apart(dve)
                    A.did(V.copy_predicated(halves(nb, 0, TOK), halves(qpos, 0, TOK), table[:, :, :, 2:2 + TOK]))
                    A.did(V.tensor_scalar(flat(q).bitcast(U32), flat(q).bitcast(U32), 0x7FFFFFFF, None,
                                          ALU.bitwise_and))
                if part == 6:
                    centre = table[:, :, :, 1:1 + TOK]
                    A.settle(g)
                    A.did(V.tensor_tensor(halves(nb, 0, TOK), halves(nb, 0, TOK), centre, ALU.subtract))
                    A.settle(g)
                    A.did(V.tensor_tensor(nb[:ROWS], q[:ROWS, :, 1:1 + TOK], nb[:ROWS], ALU.mult))
                    A.settle(g)
                    A.did(V.tensor_tensor(halves(nb, 0, TOK), halves(nb, 0, TOK), centre, ALU.add))
                if part == 7:
                    A.settle(g)
                    A.did(V.scalar_tensor_tensor(nb[:ROWS], simS[:ROWS], SCALE, nb[:ROWS], ALU.mult, ALU.add))
                    A.settle(g)
                    A.did(V.tensor_reduce(mx[:ROWS], nb[:ROWS], AX_X, ALU.max))
                    A.settle(g)
                    V.tensor_tensor(lg[:ROWS], nb[:ROWS], mx[:ROWS].unsqueeze(2).to_broadcast([ROWS, HEADS, TOK]),
                                    ALU.subtract).then_inc(logits, 1)
                    A.end()

            def attention(g):
                keep = same_img[:ROWS].rearrange("p b j -> p (b j)").unsqueeze(1).to_broadcast([ROWS, 4, ROWS])
                for s in range(4):
                    bank = (ps_g[:, s] if s < 2 else ps_t[:, s - 2])
                    dve.wait_ge(at_done, g * 4 + s + 1)
                    V.tensor_tensor(attnT[:ROWS, 4 * s:4 * s + 4],
                                    bank[:ROWS, :4 * ROWS].rearrange("p (h r) -> p h r", h=4), keep, ALU.mult
                                    ).then_inc(at_sb, 1)

            def softmax_norm(g):
                dve.wait_ge(exp_ready, g + 1)
                S.did(V.tensor_reduce(den[:ROWS], ex[:ROWS], AX_X, ALU.add))
                S.settle(g)
                S.did(V.reciprocal(rden[:ROWS], den[:ROWS]))
                S.settle(g)
                V.tensor_tensor(lg[:ROWS], ex[:ROWS], rden[:ROWS].unsqueeze(2).to_broadcast([ROWS, HEADS, TOK]),
                                ALU.mult).then_inc(weights, 1)

            def norm1(g):
                dve.wait_ge(proj_done, g + 1)
                dve.wait_ge(htok_ready, g + 1)
                V.tensor_tensor(res1[:ROWS], ps_s[:ROWS, :EMB], htok[:ROWS], ALU.add).then_inc(res1_done, 1)
                dve.wait_ge(res1_done, g + 1)
                S.did(V.bn_stats(st1[:ROWS], res1[:ROWS]))
                S.settle(g)
                apart(dve)
                S.did(V.bn_aggr(mv1[:ROWS], st1[:ROWS]))
                S.settle(g)
                V.tensor_scalar(ve1[:ROWS], mv1[:ROWS, 1:2], EPS, None, ALU.add).then_inc(var1, 1)
                if not first(g):
                    dve.wait_ge(h1_stored, g * 16 * TOPK)
                    dve.wait_ge(h1t_done, g)
                dve.wait_ge(rstd1, g + 1)
                V.tensor_scalar(h1[:ROWS], res1[:ROWS], mv1[:ROWS, 0:1], rs1[:ROWS], ALU.subtract, ALU.mult
                                ).then_inc(h1_ready, 1)
                S.end()

            def router(f, part):
                if part == 0:
                    dve.wait_ge(rout_done, f + 1)
                    F.did(V.tensor_reduce(rmax[:ROWS], ps_s[:ROWS, :NEXP], AX_X, ALU.max))
                    F.settle(f)
                    V.tensor_scalar(rlg[:ROWS], ps_s[:ROWS, :NEXP], rmax[:ROWS], None, ALU.subtract
                                    ).then_inc(rlg_ready, 1)
                if part == 1:
                    dve.wait_ge(rexp_ready, f + 1)
                    F.did(V.reciprocal(rinv[:ROWS], rsum[:ROWS]))
                    F.settle(f)
                    F.did(V.tensor_scalar(rsc[:ROWS], rexp[:ROWS], rinv[:ROWS], None, ALU.mult))
                    F.settle(f)
                    apart(dve)
                    F.did(V.max(top[:ROWS], rsc[:ROWS]))
                    F.settle(f)
                    apart(dve)
                    F.did(V.max_index(topi[:ROWS], top[:ROWS], rsc[:ROWS]))
                    F.settle(f)
                    F.did(V.tensor_copy(topf[:ROWS], topi[:ROWS]))
                    F.settle(f)
                    F.did(V.tensor_scalar(c1[:ROWS], iota8[:ROWS], topf[:ROWS, 0:1], None, ALU.is_equal))
                    F.did(V.tensor_scalar(c2[:ROWS], iota8[:ROWS], topf[:ROWS, 1:2], None, ALU.is_equal))
                    F.settle(f)
                    V.tensor_tensor(chosen[:ROWS], c1[:ROWS], c2[:ROWS], ALU.add).then_inc(chosen_ready, 1)

            def hidden_sum(f):
                dve.wait_ge(rec_stored, f * 16 + 1)
                dve.wait_ge(ids_left, f + 1)
                dve.wait_ge(ffn_done, f + 1)
                V.tensor_tensor(rec[:ROWS, :EMB], ps_acc[:ROWS, :EMB], h1[:ROWS], ALU.add).then_inc(sum_read, 1)
                F.did(V.tensor_copy(rec[:ROWS, EMB:EMB + TOPK], top[:ROWS, :TOPK]))

            def slots(f):
                dve.wait_ge(rank_done, f + 1)
                F.did(V.tensor_tensor(slot8[:ROWS], ps_s[:ROWS, EMB:EMB + NEXP], slot0[:ROWS], ALU.add))
                F.did(V.tensor_tensor(earlier[:ROWS], earlier[:ROWS], chosen[:ROWS], ALU.add))
                F.did(V.tensor_copy(ids[:ROWS, 0:1], idf[:ROWS]))
                F.did(V.tensor_scalar(ids[:ROWS, 1:2], idf[:ROWS], float(TOKENS), None, ALU.add))
                F.settle(f)
                F.did(V.tensor_tensor(pick[:ROWS, 0], c1[:ROWS], slot8[:ROWS], ALU.mult))
                F.did(V.tensor_tensor(pick[:ROWS, 1], c2[:ROWS], slot8[:ROWS], ALU.mult))
                F.did(V.tensor_scalar(idf[:ROWS], idf[:ROWS], float(ROWS), None, ALU.add))
                F.settle(f)
                F.did(V.tensor_reduce(slotf[:ROWS], pick[:ROWS], AX_X, ALU.add))
                F.settle(f)
                V.tensor_copy(slotu[:ROWS], slotf[:ROWS]).then_inc(rec_ready, 1)
                F.end()

            def hidden(f, i):
                bank = ps_g[:ROWS, (i + 1) % 2]
                dve.wait_ge(thg_ready, f * NFF + i + 1)
                F.did(V.scalar_tensor_tensor(sg[:ROWS, i % 2], thg[:ROWS, i % 2], 1.0, bank[:, :FF],
                                             ALU.add, ALU.mult))
                F.settle(f)
                V.scalar_tensor_tensor(hid[:ROWS, i % 2], sg[:ROWS, i % 2], 0.5, bank[:, FF:],
                                       ALU.mult, ALU.mult).then_inc(hid_ready, 1)

            def ffn(f, g):
                def part(n):
                    if g is not None:
                        cope(g, n)

                part(4)
                router(f, 0)
                hidden(f, 0)
                router(f, 1)
                hidden(f, 1)
                part(5)
                part(6)
                hidden_sum(f)
                part(7)
                slots(f)

            def middle(t):
                softmax_norm(t - 1)
                scores(t)
                cope(t, 0)
                attention(t - 1)
                cope(t, 1)
                cope(t, 2)
                norm1(t - 1)
                cope(t, 3)

            for free in (sum_read, rec_stored):
                dve.nop().then_inc(free, 1)

            dve.wait_ge(setup_t, 4)
            dve.wait_ge(zeroed, 3)
            V.tensor_copy(posT[:], ps_t[:, 1, :KE * (TOK + 2)].rearrange("p (m t) -> p m t", m=KE)
                          ).then_inc(tables, 1)
            dve.wait_ge(tables, 1)
            for m in range(KE):
                V.tensor_scalar(posb[:, m, 1:], posT[:, m, 1:TOK], posT[:, m, TOK:TOK + 1], None, ALU.add
                                ).then_inc(tables, 1)
                V.tensor_tensor(hT[:, m, :, 0:1], posT[:, m, 0:1].unsqueeze(1).to_broadcast([P, TPG, 1]),
                                posT[:, m, TOK + 1:].unsqueeze(1).to_broadcast([P, TPG, 1]), ALU.add
                                ).then_inc(tables, 1)
            for h in range(2):
                part = slice(DH * h, DH * h + DH)
                V.tensor_copy(cope_bd[part, h, :SL], cope_nat[part, SL - 1::-1]).then_inc(tables, 1)
            dve.wait_ge(consts, N_CONSTS)
            V.tensor_copy(own_img[:], same_img[:, :, 0]).then_inc(tables, 1)
            dve.wait_ge(tables, 8)

            embed(0)
            scores(0)
            for part in range(4):
                cope(0, part)
            embed(1)
            for part in range(4, 8):
                cope(0, part)
            middle(1)
            embed(2)

            with dve.Fori(2, G - 1) as t:
                ffn(t - 2, t - 1)
                middle(t)
                embed(t + 1)
            ffn(G - 3, G - 2)
            middle(G - 1)
            ffn(G - 2, G - 1)
            softmax_norm(G - 1)
            attention(G - 1)
            norm1(G - 1)
            ffn(G - 1, None)

            W = Steps(dve_tab, 0)
            dve.wait_ge(counted, 1)
            tiles_of, through, one8 = cnt[:, 0], cnt[:, 1], cnt[:, 2]
            W.did(V.tensor_scalar(tiles_of, ps_s[:, EMB:EMB + NEXP], (P - 1) / 2, 1.0 / P, ALU.add, ALU.mult))
            W.did(V.memset(one8, 1.0))
            W.settle(0)
            W.did(V.tensor_scalar(tiles_of, tiles_of, RNE, -RNE, ALU.add, ALU.add))
            W.settle(0)
            W.did(V.tensor_tensor_scan(through, one8, tiles_of, 0.0, ALU.mult, ALU.add))
            W.settle(0)
            by_tile = [P, NT, NEXP]
            W.did(V.tensor_tensor(past[:], tile_no[:].unsqueeze(2).to_broadcast(by_tile),
                                  through.unsqueeze(1).to_broadcast(by_tile), ALU.is_ge))
            W.settle(0)
            W.did(V.tensor_reduce(tl[:, 0], past[:], AX_X, ALU.add))
            W.settle(0)
            W.did(V.tensor_tensor(past[:], past[:], tiles_of.unsqueeze(1).to_broadcast(by_tile), ALU.mult))
            W.settle(0)
            W.did(V.tensor_reduce(tl[:, 1], past[:], AX_X, ALU.add))
            W.settle(0)
            W.did(V.tensor_tensor(tl[:, 1], tile_no[:], tl[:, 1], ALU.subtract))
            W.did(V.tensor_scalar(tl[:, 2], tl[:, 0], float(CAP), None, ALU.mult))
            W.settle(0)
            W.did(V.scalar_tensor_tensor(tl[:, 2], tl[:, 1], float(P), tl[:, 2], ALU.mult, ALU.add))
            W.did(V.tensor_scalar(tl[:, 0], tl[:, 0], float(NEXP - 1), None, ALU.min))
            W.settle(0)
            W.did(V.tensor_copy(tile_slot[:], tl[:, 2]))
            W.did(V.tensor_copy(tile_expert[:], tl[:, 0]))
            W.settle(0)
            V.nop().then_inc(tiles_ready, 1)
            def hidden_tile(t, i):
                dve.wait_ge(tile_tanh, t + 1)
                V.scalar_tensor_tensor(sg[:, i], thg[:, i], 1.0, ps_g[:, i, :FF], ALU.add, ALU.mult
                                       ).then_inc(dve_tile, 1)
                dve.wait_ge(dve_tile, t + 1)
                V.scalar_tensor_tensor(hid[:, i], sg[:, i], 0.5, ps_g[:, i, FF:], ALU.mult, ALU.mult
                                       ).then_inc(tile_hid, 1)

            def y_tile(t, turn, b):
                if turn is not None:
                    dve.wait_ge(tile_stored[(b + 2) % 4], turn * 16)
                dve.wait_ge(tile_y, t + 1)
                V.tensor_copy(y_sb[:, b % 2], ps_e[:, b % 2, :EMB]).then_inc(tile_y_sb, 1)

            hidden_tile(0, 0)
            for t in range(4):
                hidden_tile(t + 1, (t + 1) % 2)
                y_tile(t, 1 if t >= 2 else None, t)
            with dve.Fori(1, NT // 4) as four:
                for b in range(4):
                    hidden_tile(four * 4 + b + 1, (b + 1) % 2)
                    y_tile(four * 4 + b, four + b // 2, b)
            hidden_tile(NT - 1, 1)
            y_tile(NT - 2, NT // 4, 0)
            y_tile(NT - 1, NT // 4, 1)

            L = Steps(dve_last, 4)

            def add_experts(turn, b):
                g = turn * NB + b
                dve.wait_ge(rec_in[b], (turn + 1) * 16 * (1 + TOPK))
                res = resc[:ROWS, b]
                L.did(V.scalar_tensor_tensor(res, yc[:ROWS, b, 0], recc[:ROWS, b, EMB:EMB + 1],
                                             recc[:ROWS, b, :EMB], ALU.mult, ALU.add))
                L.settle(g)
                L.did(V.scalar_tensor_tensor(res, yc[:ROWS, b, 1], recc[:ROWS, b, EMB + 1:EMB + 2], res,
                                             ALU.mult, ALU.add))
                L.settle(g)
                apart(dve)
                L.did(V.bn_stats(stc[:ROWS, b], res))
                L.settle(g)
                apart(dve)
                L.did(V.bn_aggr(mvc[:ROWS, b], stc[:ROWS, b]))
                L.settle(g)
                V.tensor_scalar(vec[:ROWS, bass.ds(g, 1)], mvc[:ROWS, b, 1:2], EPS, None, ALU.add).then_inc(var2, 1)
                L.end()

            def norm2(turn, b):
                g = turn * NB + b
                if not first(turn):
                    dve.wait_ge(stored[b], turn * 32)
                dve.wait_ge(rstd2, g + 1)
                V.tensor_scalar(outc[:ROWS, b], resc[:ROWS, b], mvc[:ROWS, b, 0:1], rsc2[:ROWS, bass.ds(g, 1)],
                                ALU.subtract, ALU.mult).then_inc(out_ready, 1)

            add_experts(0, 0)
            for g in range(NB):
                add_experts((g + 1) // NB, (g + 1) % NB)
                norm2(0, g)
            with dve.Fori(1, (G - 2) // NB) as four:
                for b in range(NB):
                    add_experts(four + (b + 1) // NB, (b + 1) % NB)
                    norm2(four, b)
            add_experts((G - 1) // NB, (G - 1) % NB)
            for g in range(G - 2, G):
                norm2(g // NB, g % NB)


_INS = ['x', 'L0_tok_W', 'L0_tok_b', 'L0_tok_cls_token', 'L0_tok_pos_embed', 'L0_attn_Wq', 'L0_attn_Wkv',
        'L0_attn_Wout', 'L0_attn_b_out', 'L0_attn_pos_emb', 'L0_ffn_router_w', 'L0_ffn_gate_w', 'L0_ffn_up_w',
        'L0_ffn_down_w', 'L0_ffn_shared_gate_w', 'L0_ffn_shared_up_w', 'L0_ffn_shared_down_w']
_OUTS = [((64, 37, 256), 'float32')]


def kernel(**inputs):
    import numpy as _np
    import concourse.bacc as _bacc
    from concourse import mybir as _mybir
    from concourse.bass_utils import run_bass_kernel_spmd as _run

    nc = _bacc.Bacc("TRN2", target_bir_lowering=False, num_devices=1)
    arrays, args = {}, []
    for name in _INS:
        a = _np.ascontiguousarray(inputs[name])
        arrays[f"in_{name}_dram"] = a
        args.append(nc.dram_tensor(f"in_{name}_dram", a.shape, _mybir.dt.from_np(a.dtype), kind="ExternalInput").ap())
    for i, (shape, dtype) in enumerate(_OUTS):
        dt = _mybir.dt.from_np(_np.dtype(dtype))
        args.append(nc.dram_tensor(f"out_{i}_dram", shape, dt, kind="ExternalOutput").ap())
    vit_tower(nc, *args)
    r = _run(nc, [arrays], core_ids=[0])
    got = tuple(r.results[0][f"out_{i}_dram"] for i in range(len(_OUTS)))
    return got[0]
```

```python
from contextlib import ExitStack

import concourse.bass as bass
from concourse import mybir

ALU = mybir.AluOpType
ACT = mybir.ActivationFunctionType
F32 = mybir.dt.float32
I16 = mybir.dt.int16
I32 = mybir.dt.int32
U32 = mybir.dt.uint32
AX_X = mybir.AxisListType.X


def vit_tower(nc, x, tok_w, tok_b, cls_token, pos_embed, wq, wkv, wout, b_out, cope_emb,
              router_w, gate_w, up_w, down_w, sh_gate_w, sh_up_w, sh_down_w, out):
    P = 128
    IMGS, CH, SIDE, _ = x.shape
    EMB, PD = tok_w.shape
    TOK = pos_embed.shape[1]
    PATCH = 16
    NPH = SIDE // PATCH
    KE = EMB // P
    KP = PD // P
    INNER = wq.shape[1]
    DH = cope_emb.shape[0]
    HEADS = INNER // DH
    FT = INNER // P
    NEXP, _, FF = gate_w.shape
    SH = sh_gate_w.shape[1] // FF
    TOPK = 2
    TPG = 3
    ROWS = TPG * TOK
    G = -(-IMGS // TPG)
    XR = TPG * CH * NPH
    NPAT = TPG * NPH * NPH
    SL = TOK + 2
    SLP = 48
    HB = HEADS // 2
    SCALE = float(DH) ** -0.5
    RNE = 12582912.0
    EPS = 1e-5
    SHIFTS = [32, 16, 8, 4, 2]
    REC = EMB + TOPK
    TOKENS = G * ROWS
    CAP = -(-G * ROWS // P) * P
    NT = (TOPK * G * ROWS - NEXP) // P + NEXP
    SLOTS = NEXP * CAP + NT * P
    assert NT % 4 == 2 and NEXP == 8 and SLOTS % P == 0 and G % 4 == 2
    assert TOK + 1 < 64 and FF == 256 and EMB == 256 and ROWS <= P

    with ExitStack() as ctx:
        def sb(name, shape, dt=F32):
            return ctx.enter_context(nc.sbuf_tensor(name, shape, dt))

        def sem(name):
            return ctx.enter_context(nc.semaphore(name))

        tokT = sb("tokT", [P, KP, EMB])
        wq_sb = sb("wq_sb", [P, KE, INNER])
        wkv_sb = sb("wkv_sb", [P, KE, 2 * INNER])
        wout_sb = sb("wout_sb", [P, FT, EMB])
        gu_sb = sb("gu_sb", [P, NEXP, KE, 2, FF])
        down_sb = sb("down_sb", [P, NEXP, KE, EMB])
        sgu_sb = sb("sgu_sb", [P, SH, KE, 2, FF])
        sdown_sb = sb("sdown_sb", [P, SH * KE, EMB])
        rw_sb = sb("rw_sb", [P, KE, NEXP])
        bout_b = sb("bout_b", [P, EMB])
        pe_nat = sb("pe_nat", [TOK + 2, EMB])
        posT = sb("posT", [P, KE, TOK + 2])
        cope_nat = sb("cope_nat", [P, DH])
        ident = sb("ident", [P, P])
        same_img = sb("same_img", [P, TPG, TOK])
        own_img = sb("own_img", [P, TPG], I16)
        cope_bd = sb("cope_bd", [P, 2, SLP])
        posb = sb("posb", [P, KE, TOK])
        scan_keep = sb("scan_keep", [P, HEADS, SL])
        iota8 = sb("iota8", [P, NEXP])
        neg_half = sb("neg_half", [P, 1])
        x_sb = sb("x_sb", [XR, PATCH * SIDE])
        xp_sb = sb("xp_sb", [XR, NPH, PATCH * PATCH])
        patT = sb("patT", [P, 2, NPH, XR])
        hT = sb("hT", [P, KE, TPG, TOK])
        htok = sb("htok", [P, EMB])
        qT = sb("qT", [P, FT, ROWS])
        qBD = sb("qBD", [P, FT, 2, ROWS])
        kT = sb("kT", [P, FT, ROWS])
        v_sb = sb("v_sb", [P, INNER])
        th = sb("th", [P, HEADS, TOK])
        simS = sb("simS", [P, HEADS, TOK])
        gate = sb("gate", [P, HEADS, SL])
        u = sb("u", [P, HEADS, SL])
        rr = sb("rr", [P, HEADS, SL])
        dI = sb("dI", [P, HEADS, SL], I16)
        dE = sb("dE", [P, HEADS, SL], I16)
        bit = sb("bit", [P, len(SHIFTS), HEADS, SL], I16)
        q = rr
        qpos = sb("qpos", [P, HEADS, TOK], I16)
        nb = sb("nb", [P, HEADS, TOK])
        lg = sb("lg", [P, HEADS, TOK])
        ex = sb("ex", [P, HEADS, TOK])
        attn = sb("attn", [P, HEADS, TPG, TOK])
        mx = sb("mx", [P, HEADS])
        w_nat = attn[:].rearrange("p h b j -> p (h b j)")[:, :KE * PD].rearrange("p (t d) -> p t d", t=KE)
        den = sb("den", [P, HEADS])
        rden = sb("rden", [P, HEADS])
        attnT = sb("attnT", [P, HEADS, ROWS])
        up = sb("up", [P, HEADS, SL])
        oT = sb("oT", [P, FT, ROWS])
        res1 = sb("res1", [P, EMB])
        h1 = sb("h1", [P, EMB])
        h1T = sb("h1T", [P, KE, ROWS])
        st1 = sb("st1", [P, 6])
        mv1 = sb("mv1", [P, 2])
        ve1 = sb("ve1", [P, 1])
        rs1 = sb("rs1", [P, 1])
        rmax = sb("rmax", [P, 1])
        rlg = sb("rlg", [P, NEXP])
        rexp = sb("rexp", [P, NEXP])
        rsum = sb("rsum", [P, 1])
        rinv = sb("rinv", [P, 1])
        rsc = sb("rsc", [P, NEXP])
        top = sb("top", [P, 8])
        topi = sb("topi", [P, 8], U32)
        topf = sb("topf", [P, 8])
        c1 = sb("c1", [P, NEXP])
        c2 = sb("c2", [P, NEXP])
        chosen = sb("chosen", [P, NEXP])
        earlier = sb("earlier", [P, NEXP])
        slot8 = sb("slot8", [P, NEXP])
        pick = sb("pick", [P, TOPK, NEXP])
        slotf = sb("slotf", [P, TOPK])
        idf = sb("idf", [P, 1])
        ids = sb("ids", [P, TOPK], U32)
        rec = sb("rec", [P, REC])
        slotu = sb("slotu", [P, TOPK], U32)
        thg = sb("thg", [P, 2, FF])
        sg = sb("sg", [P, 2, FF])
        hid = sb("hid", [P, 2, FF])
        hidT = sb("hidT", [P, 2, KE, P])
        earlier_than = sb("earlier_than", [P, P])
        ones = sb("ones", [P, P])
        slot0 = sb("slot0", [P, NEXP])
        no_ids = sb("no_ids", [P, SLOTS // P], U32)
        tile_no = sb("tile_no", [P, NT])
        past = sb("past", [P, NT, NEXP])
        cnt = sb("cnt", [P, 3, NEXP])
        tl = sb("tl", [P, 3, NT])
        AT_ONCE = 6
        names = sb("names", [P, NT // 4])
        tile_experts = sb("tile_experts", [P, NT // 4], I32)
        tile_slot = sb("tile_slot", [P, NT], I32)
        ids_in = sb("ids_in", [P, 4], U32)
        ids_t = sb("ids_t", [P, 4], U32)
        ids_y = sb("ids_y", [P, 4], U32)
        spare = attnT[:].rearrange("p h r -> p (h r)")
        xgT = spare[:, :4 * P].rearrange("p (i k r) -> p i k r", i=2, k=KE)
        y_sb = spare[:, 4 * P:4 * P + 2 * EMB].rearrange("p (i e) -> p i e", i=2)
        xg = attn[:].rearrange("p h b j -> p (h b j)")[:, :4 * EMB].rearrange("p (b e) -> p b e", b=4)
        NB = 4
        last_a = wkv_sb[:].rearrange("p k n -> p (k n)")
        yc = last_a[:, :2 * NB * EMB].rearrange("p (b j e) -> p b j e", b=NB, j=TOPK)
        resc = last_a[:, 2 * NB * EMB:3 * NB * EMB].rearrange("p (b e) -> p b e", b=NB)
        outc = last_a[:, 3 * NB * EMB:].rearrange("p (b e) -> p b e", b=NB)
        recc = wq_sb[:].rearrange("p k n -> p (k n)")[:, :NB * REC].rearrange("p (b e) -> p b e", b=NB)
        stc = sb("stc", [P, NB, 6])
        mvc = sb("mvc", [P, NB, 2])
        vec = sb("vec", [P, G])
        rsc2 = sb("rsc2", [P, G])

        h1_d = nc.dram_tensor("h1_d", [TOPK * TOKENS, EMB], F32, kind="Internal").ap()
        rec_d = nc.dram_tensor("rec_d", [TOKENS, REC], F32, kind="Internal").ap()
        ids_d = nc.dram_tensor("ids_d", [SLOTS, 1], U32, kind="Internal").ap()
        y_d = nc.dram_tensor("y_d", [TOPK * TOKENS, EMB], F32, kind="Internal").ap()

        ps_g = ctx.enter_context(nc.psum_tensor("ps_g", [P, 2, 512], F32))
        ps_t = ctx.enter_context(nc.psum_tensor("ps_t", [P, 2, 512], F32))
        ps_e = ctx.enter_context(nc.psum_tensor("ps_e", [P, 2, 512], F32))
        ps_s = ctx.enter_context(nc.psum_tensor("ps_s", [P, 512], F32))
        ps_acc = ctx.enter_context(nc.psum_tensor("ps_acc", [P, 512], F32))

        w_tok = sem("w_tok")
        w_q = sem("w_q")
        w_kv = sem("w_kv")
        w_o = sem("w_o")
        w_ffn = sem("w_ffn")
        w_exp = sem("w_exp")
        w_small = sem("w_small")
        zeroed = sem("zeroed")
        consts = sem("consts")
        setup_t = sem("setup_t")
        setup_sb = sem("setup_sb")
        tables = sem("tables")
        x_in = sem("x_in")
        xp_ready = sem("xp_ready")
        xt_done = sem("xt_done")
        xt_sb = sem("xt_sb")
        emb_done = sem("emb_done")
        hT_ready = sem("hT_ready")
        qk_done = sem("qk_done")
        qk_sb = sem("qk_sb")
        sim_done = sem("sim_done")
        tanh_sb = sem("tanh_sb")
        sim_first = sem("sim_first")
        sim_sb = sem("sim_sb")
        cope_done = sem("cope_done")
        v_done = sem("v_done")
        v_ready = sem("v_ready")
        ht_done = sem("ht_done")
        ht_sb = sem("ht_sb")
        htok_ready = sem("htok_ready")
        logits = sem("logits")
        exp_ready = sem("exp_ready")
        weights = sem("weights")
        attn_ready = sem("attn_ready")
        at_done = sem("at_done")
        at_sb = sem("at_sb")
        o_done = sem("o_done")
        ot_sb = sem("ot_sb")
        proj_done = sem("proj_done")
        res1_done = sem("res1_done")
        var1 = sem("var1")
        rstd1 = sem("rstd1")
        h1_ready = sem("h1_ready")
        h1t_done = sem("h1t_done")
        h1t_sb = sem("h1t_sb")
        rout_done = sem("rout_done")
        rlg_ready = sem("rlg_ready")
        rexp_ready = sem("rexp_ready")
        gu_done = sem("gu_done")
        thg_ready = sem("thg_ready")
        hid_ready = sem("hid_ready")
        hidt_done = sem("hidt_done")
        hidt_sb = sem("hidt_sb")
        ffn_done = sem("ffn_done")
        chosen_ready = sem("chosen_ready")
        rank_done = sem("rank_done")
        sum_read = sem("sum_read")
        slots_ready = sem("slots_ready")
        rec_ready = sem("rec_ready")
        h1_stored = sem("h1_stored")
        rec_stored = sem("rec_stored")
        ids_stored = sem("ids_stored")
        ids_left = sem("ids_left")
        ids_zeroed = sem("ids_zeroed")
        counted = sem("counted")
        tiles_ready = sem("tiles_ready")
        ids_taken = sem("ids_taken")
        ids_kept = sem("ids_kept")
        xg_zeroed = sem("xg_zeroed")
        tile_ids = [sem(f"tile_ids_{i}") for i in range(4)]
        tile_x = [sem(f"tile_x_{i}") for i in range(4)]
        tile_xt = sem("tile_xt")
        tile_xt_sb = sem("tile_xt_sb")
        tile_gu = sem("tile_gu")
        tile_tanh = sem("tile_tanh")
        tile_hid = sem("tile_hid")
        tile_hidt = sem("tile_hidt")
        tile_hidt_sb = sem("tile_hidt_sb")
        tile_y = sem("tile_y")
        tile_y_sb = sem("tile_y_sb")
        tile_stored = [sem(f"tile_stored_{i}") for i in range(4)]
        rec_in = [sem(f"rec_in_{i}") for i in range(NB)]
        var2 = sem("var2")
        rstd2 = sem("rstd2")
        out_ready = sem("out_ready")
        stored = [sem(f"stored_{i}") for i in range(NB)]
        dve_tab = sem("dve_tab")
        dve_tile = sem("dve_tile")
        dve_last = sem("dve_last")
        dve_attn = sem("dve_attn")
        dve_soft = sem("dve_soft")
        dve_ffn = sem("dve_ffn")
        DVE_ATTN = 24
        DVE_SOFT = 4
        DVE_FFN = 18

        NFF = SH

        N_CONSTS = 17

        def first(g):
            return isinstance(g, int) and g == 0

        x_rows = x.rearrange("b c (r i) w -> (b c r) (i w)", i=PATCH)
        out_rows = out.rearrange("b t e -> (b t) e")

        def split(t, a0, a1):
            return t[:ROWS, :, a0:a1].rearrange("p (k h) a -> p k h a", h=4)

        def halves(t, a0, a1):
            return t[:ROWS, :, a0:a1].rearrange("p (k h) a -> p k h a", h=HB)

        def apart(eng):
            eng.nop(nofuse=True)

        block = ctx.enter_context(nc.Block())

        @block.sync
        def _(sp):
            def load_x(g, row):
                if not first(g):
                    sp.wait_ge(xp_ready, g)
                sp.dma_start(x_sb[:, :], x_rows[bass.ds(row, XR), :]).then_inc(x_in, 16)

            def store_rows(g, row):
                sp.wait_ge(h1_ready, g + 1)
                for j in range(TOPK):
                    sp.dma_start(h1_d[bass.ds(row + j * TOKENS, ROWS), :], h1[:ROWS]).then_inc(h1_stored, 16)

            def store_rec(g, row):
                sp.wait_ge(rec_ready, g + 1)
                sp.dma_start(rec_d[bass.ds(row, ROWS), :], rec[:ROWS]).then_inc(rec_stored, 16)

            sp.dma_start(w_nat[:, :, :], tok_w.rearrange("(t p) d -> p t d", p=P)).then_inc(w_tok, 16)
            load_x(0, 0)
            sp.dma_start(pe_nat[:TOK, :], pos_embed[0]).then_inc(w_small, 16)
            sp.dma_start(pe_nat[TOK:TOK + 1, :], tok_b.rearrange("(a e) -> a e", a=1)).then_inc(w_small, 16)
            sp.dma_start(pe_nat[TOK + 1:, :], cls_token[0]).then_inc(w_small, 16)
            for h in range(2):
                sp.dma_start(cope_nat[DH * h:DH * h + DH, :], cope_emb).then_inc(w_small, 16)
            sp.dma_start(wq_sb[:, :, :], wq.rearrange("(t p) n -> p t n", p=P)).then_inc(w_q, 16)
            sp.dma_start(wkv_sb[:, :, :], wkv.rearrange("(t p) n -> p t n", p=P)).then_inc(w_kv, 16)
            sp.dma_start(wout_sb[:, :, :], wout.rearrange("(t p) n -> p t n", p=P)).then_inc(w_o, 16)
            load_x(1, XR)
            sp.dma_start(bout_b[:, :], b_out.partition_broadcast(P)).then_inc(w_o, 16)
            sp.dma_start(rw_sb[:, :, :], router_w.rearrange("(t p) e -> p t e", p=P)).then_inc(w_ffn, 16)
            for t in range(KE):
                rows = slice(P * t, P * t + P)
                for j, w in enumerate((sh_gate_w, sh_up_w)):
                    sp.dma_start(sgu_sb[:, :, t, j, :], w[rows, :].rearrange("p (s f) -> p s f", f=FF)
                                 ).then_inc(w_ffn, 16)
            sp.dma_start(sdown_sb[:, :, :], sh_down_w.rearrange("(t p) n -> p t n", p=P)).then_inc(w_ffn, 16)
            load_x(2, 2 * XR)
            for t in range(KE):
                rows = slice(P * t, P * t + P)
                for j, w in enumerate((gate_w, up_w)):
                    sp.dma_start(gu_sb[:, :, t, j, :], w[:, rows, :].rearrange("e p f -> p e f")
                                 ).then_inc(w_exp, 16)
                sp.dma_start(down_sb[:, :, t, :], down_w[:, rows, :].rearrange("e p n -> p e n")
                             ).then_inc(w_exp, 16)

            sp.wait_ge(consts, N_CONSTS)
            sp.dma_start(ids_d.rearrange("(p n) o -> p (n o)", p=P), no_ids[:, :]).then_inc(ids_zeroed, 16)
            with sp.Fori(2, G - 2) as t:
                load_x(t + 1, (t + 1) * XR)
                store_rows(t - 2, (t - 2) * ROWS)
                store_rec(t - 2, (t - 2) * ROWS)
            load_x(G - 1, (IMGS - TPG) * CH * NPH)
            for g in range(G - 4, G):
                store_rows(g, g * ROWS)
                if g < G - 1:
                    store_rec(g, g * ROWS)

            def load_ids(t, b):
                slot = nc.sync.value_load(tile_slot[0:1, bass.ds(t, 1)], min_val=0, max_val=SLOTS - P)
                sp.dma_start(ids_in[:, b:b + 1], ids_d[bass.ds(slot, P), :]).then_inc(tile_ids[b], 16)

            sp.wait_ge(tiles_ready, 1)
            sp.wait_ge(ids_stored, 16 * TOPK * G)
            for t in range(4):
                load_ids(t, t)
            store_rec(G - 1, (G - 1) * ROWS)
            with sp.Fori(0, NT // 4 - 1) as four:
                for b in range(4):
                    t = four * 4 + b
                    sp.wait_ge(ids_taken, t + 1)
                    load_ids(t + 4, b)
            for t in range(NT - 6, NT - 4):
                sp.wait_ge(ids_taken, t + 1)
                load_ids(t + 4, t % 4)

            by_token = y_d.rearrange("(j n) e -> n j e", j=TOPK)

            def load_rec(g, row, b):
                sp.dma_start(recc[:ROWS, b], rec_d[bass.ds(row, ROWS), :]).then_inc(rec_in[b], 16)
                sp.dma_start(yc[:ROWS, b], by_token[bass.ds(row, ROWS)]).then_inc(rec_in[b], 16)

            sp.wait_ge(rec_stored, 16 * G + 1)
            for b in range(4):
                sp.wait_ge(tile_stored[b], 16 * -(-(NT - b) // 4))
            for g in range(NB):
                load_rec(g, g * ROWS, g)
            with sp.Fori(1, G // NB) as four:
                for b in range(NB):
                    g = four * NB + b
                    if b % 2 == 0:
                        sp.wait_ge(var2, four * 2 - 1 + b // 2)
                    load_rec(g, g * ROWS, b)
            for g in range(G // NB * NB, G):
                sp.wait_ge(var2, g // 2 - 1)
                load_rec(g, g * ROWS, g % NB)
            sp.wait_ge(h1_stored, 16 * TOPK * G)

        N_W_FFN = 16 * (2 + 2 * KE)
        N_W_EXP = 16 * 3 * KE

        @block.gpsimd
        def _(pool):
            for buf in (qBD, cope_bd, gate):
                nc.gpsimd.memset(buf[:], 0.0).then_inc(zeroed, 1)
            nc.gpsimd.memset(scan_keep[:], 1.0).then_inc(consts, 1)
            nc.gpsimd.memset(ident[:], 1.0).then_inc(consts, 1)
            nc.gpsimd.memset(same_img[:], 1.0).then_inc(consts, 1)
            nc.gpsimd.memset(neg_half[:], -0.5).then_inc(consts, 1)
            nc.gpsimd.iota(iota8[:], pattern=[[1, NEXP]], base=0, channel_multiplier=0,
                           allow_small_or_imprecise_dtypes=True).then_inc(consts, 1)
            nc.gpsimd.memset(ones[:], 1.0).then_inc(consts, 1)
            nc.gpsimd.memset(earlier_than[:], 1.0).then_inc(consts, 1)
            nc.gpsimd.memset(earlier[:], 0.0).then_inc(consts, 1)
            nc.gpsimd.memset(no_ids[:], TOPK * TOKENS).then_inc(consts, 1)
            for table, pattern, row in ((slot0, [[CAP, NEXP]], 0), (tile_no, [[1, NT]], 0), (idf, [[0, 1]], 1)):
                nc.gpsimd.iota(table[:], pattern=pattern, base=0, channel_multiplier=row,
                               allow_small_or_imprecise_dtypes=True).then_inc(consts, 1)
            pool.wait_ge(consts, 12)
            nc.gpsimd.affine_select(out=ident[:], in_=ident[:], compare_op=ALU.is_equal, fill=0.0, base=0,
                                    pattern=[[-1, P]], channel_multiplier=1).then_inc(consts, 1)
            nc.gpsimd.affine_select(out=same_img[:], in_=same_img[:], compare_op=ALU.is_ge, fill=0.0, base=0,
                                    pattern=[[-TOK, TPG], [0, TOK]], channel_multiplier=1).then_inc(consts, 1)
            nc.gpsimd.memset(scan_keep[:, :, SL - 1:SL], 0.0).then_inc(consts, 1)
            nc.gpsimd.affine_select(out=earlier_than[:], in_=earlier_than[:], compare_op=ALU.is_gt, fill=0.0, base=0,
                                    pattern=[[1, P]], channel_multiplier=-1).then_inc(consts, 1)
            pool.wait_ge(consts, 16)
            nc.gpsimd.affine_select(out=same_img[:], in_=same_img[:], compare_op=ALU.is_ge, fill=0.0,
                                    base=TOK - 1, pattern=[[TOK, TPG], [0, TOK]],
                                    channel_multiplier=-1).then_inc(consts, 1)

            def regroup(g):
                pool.wait_ge(x_in, g * 16 + 16)
                if not first(g):
                    pool.wait_ge(xt_done, g * 2)
                apart(pool)
                nc.gpsimd.tensor_copy(xp_sb[:, :, :].rearrange("p r (i w) -> p r i w", w=PATCH),
                                      x_sb[:, :].rearrange("p (i r w) -> p r i w", r=NPH, w=PATCH)
                                      ).then_inc(xp_ready, 1)

            def stage1(g):
                pool.wait_ge(ht_sb, g + 1)
                if first(g):
                    pool.wait_ge(w_o, 32)
                nc.gpsimd.tensor_tensor(htok[:ROWS], htok[:ROWS], bout_b[:ROWS], ALU.add).then_inc(htok_ready, 1)

            def norm(g, var, ve, rs, rstd):
                pool.wait_ge(var, g + 1)
                nc.gpsimd.tensor_tensor(rs[:ROWS], ve[:ROWS], neg_half[:ROWS], ALU.pow).then_inc(rstd, 1)

            def scatter(f):
                pool.wait_ge(slots_ready, f + 1)
                apart(pool)
                for j in range(TOPK):
                    nc.gpsimd.indirect_dma_start(
                        ids_d[:, :], bass.IndirectOffsetOnAxis(ap=slotu[:ROWS, j:j + 1], axis=0),
                        ids[:ROWS, j:j + 1], None).then_inc(ids_stored, 16)

            def numbers_left(f):
                if not first(f):
                    pool.wait_ge(ids_stored, f * 16 * TOPK)
                apart(pool)
                pool.nop().then_inc(ids_left, 1)

            regroup(0)
            regroup(1)
            stage1(0)
            pool.wait_ge(ids_zeroed, 16)

            def middle(t):
                if not isinstance(t, int) or t < G - 1:
                    regroup(t + 1)
                norm(t - 1, var1, ve1, rs1, rstd1)
                stage1(t)
                numbers_left(t - 1)
                scatter(t - 1)

            middle(1)
            with pool.Fori(2, G - 1) as t:
                middle(t)
            middle(G - 1)
            norm(G - 1, var1, ve1, rs1, rstd1)
            numbers_left(G - 1)
            scatter(G - 1)

            LAST_ID = TOPK * TOKENS - 1

            def gather_x(t, turn, b):
                pool.wait_ge(tile_ids[b], turn * 16 + 16)
                apart(pool)
                nc.gpsimd.tensor_copy(ids_t[:, b:b + 1], ids_in[:, b:b + 1]).then_inc(ids_taken, 1)
                pool.wait_ge(ids_taken, t + 1)
                apart(pool)
                nc.gpsimd.indirect_dma_start(xg[:, b], None, h1_d[:, :],
                                             bass.IndirectOffsetOnAxis(ap=ids_t[:, b:b + 1], axis=0),
                                             bounds_check=LAST_ID, oob_is_err=False).then_inc(tile_x[b], 16)

            def keep_ids(t, turn, b):
                pool.wait_ge(tile_x[b], turn * 16 + 16)
                if not first(turn):
                    pool.wait_ge(tile_stored[b], turn * 16)
                apart(pool)
                nc.gpsimd.tensor_copy(ids_y[:, b:b + 1], ids_t[:, b:b + 1]).then_inc(ids_kept, 1)
                pool.wait_ge(ids_kept, t + 1)

            def scatter_y(t, b):
                pool.wait_ge(tile_y_sb, t + 1)
                apart(pool)
                nc.gpsimd.indirect_dma_start(y_d[:, :], bass.IndirectOffsetOnAxis(ap=ids_y[:, b:b + 1], axis=0),
                                             y_sb[:, b % 2], None, bounds_check=LAST_ID, oob_is_err=False
                                             ).then_inc(tile_stored[b], 16)

            pool.wait_ge(h1_stored, 16 * TOPK * G)
            nc.gpsimd.memset(xg[:], 0.0).then_inc(xg_zeroed, 1)
            pool.wait_ge(xg_zeroed, 1)
            def ahead(t, turn, b):
                keep_ids(t, turn, b)
                pool.wait_ge(tile_xt, t + 1)
                gather_x(t + 4, turn + 1, b)

            for t in range(4):
                gather_x(t, 0, t)
            for t in range(2):
                ahead(t, 0, t)
            for t in range(4):
                ahead(t + 2, (t + 2) // 4, (t + 2) % 4)
                scatter_y(t, t)
            with pool.Fori(1, NT // 4 - 1) as four:
                for b in range(4):
                    ahead(four * 4 + b + 2, four + (b + 2) // 4, (b + 2) % 4)
                    scatter_y(four * 4 + b, b)
            for t in range(NT - 6, NT):
                if t + 2 < NT:
                    keep_ids(t + 2, (t + 2) // 4, (t + 2) % 4)
                scatter_y(t, t % 4)

            def norm_last(pair):
                pool.wait_ge(var2, pair + 1)
                of = bass.ds(pair * 2, 2)
                nc.gpsimd.tensor_tensor(rsc2[:ROWS, of], vec[:ROWS, of], neg_half[:ROWS].to_broadcast([ROWS, 2]),
                                        ALU.pow).then_inc(rstd2, 1)

            with pool.Fori(0, G // 2) as t:
                norm_last(t)

        @block.tensor
        def _(pe):
            def patches(g):
                if not first(g):
                    pe.wait_ge(v_ready, g * 2 - 1)
                if not isinstance(g, int) or g > 1:
                    pe.wait_ge(res1_done, g - 1)
                pe.wait_ge(xp_ready, g + 1)
                apart(pe)
                for half, bank in enumerate([ps_s, ps_acc]):
                    for c in range(NPH):
                        mm = nc.tensor.transpose(bank[:, c * XR:(c + 1) * XR],
                                                 xp_sb[:, c, P * half:P * half + P], ident[:XR, :XR])
                    mm.then_inc(xt_done, 1)

            def embed(g):
                pe.wait_ge(xt_sb, g * 2 + 2)
                pt = patT[:, :, :, :].rearrange("p h c (b k r) -> p h c b k r", b=TPG, k=CH)
                for m in range(KE):
                    for k in range(KP):
                        mm = nc.tensor.matmul(ps_t[:, 0, m * NPAT:(m + 1) * NPAT], tokT[:, k, m * P:(m + 1) * P],
                                              pt[:, k % 2, :, :, k // 2, :], start=(k == 0), stop=(k == KP - 1))
                mm.then_inc(emb_done, 1)

            def qk(g, s):
                if s == 0:
                    pe.wait_ge(hT_ready, (g + 1) * KE)
                    if not first(g):
                        pe.wait_ge(ht_sb, g)
                        pe.wait_ge(v_ready, g * 2)
                    else:
                        pe.wait_ge(w_q, 16)
                        pe.wait_ge(w_kv, 16)
                bank = [ps_t[:, 1], ps_g[:, 0], ps_g[:, 1], ps_t[:, 0]][s]
                w = wq_sb if s < 2 else wkv_sb
                for f in range(4):
                    c = (4 * (s % 2) + f) * P
                    for k in range(KE):
                        mm = nc.tensor.matmul(bank[:, f * ROWS:(f + 1) * ROWS], w[:, k, c:c + P],
                                              hT[:, k], start=(k == 0), stop=(k == KE - 1))
                mm.then_inc(qk_done, 1)

            def score(g):
                for s, banks in enumerate([ps_g, ps_t]):
                    pe.wait_ge(qk_sb, g * 4 + 3 + s)
                    for i in range(HB):
                        h = HB * s + i
                        mm = nc.tensor.matmul(banks[:ROWS, i // 4, i % 4 * ROWS:(i % 4 + 1) * ROWS],
                                              qBD[:, h // 2, h % 2], kT[:, h // 2], start=True, stop=True)
                    mm.then_inc(sim_done, 1)

            def v_part(g, s):
                if s == 0 and not first(g):
                    pe.wait_ge(sum_read, g)
                bank = [ps_acc, ps_g[:, 1]][s]
                for k in range(KE):
                    mm = nc.tensor.matmul(bank[:ROWS], hT[:, k],
                                          wkv_sb[:, k, INNER + 512 * s:INNER + 512 * s + 512],
                                          start=(k == 0), stop=(k == KE - 1))
                mm.then_inc(v_done, 1)

            def cope_tables(g):
                for f in range(FT):
                    c = f % 4 * 2 * SLP
                    mm = nc.tensor.matmul(ps_e[:ROWS, f // 4, c:c + 2 * SLP], qT[:, f], cope_bd[:, :, :],
                                          start=True, stop=True)
                mm.then_inc(cope_done, 1)

            def h_by_tokens(g):
                for k in range(KE):
                    mm = nc.tensor.transpose(ps_t[:ROWS, 1, k * P:(k + 1) * P],
                                             hT[:, k].rearrange("p b t -> p (b t)"), ident[:])
                mm.then_inc(ht_done, 1)

            def normed(f):
                pe.wait_ge(h1_ready, f + 1)
                for k in range(KE):
                    mm = nc.tensor.transpose(ps_g[:, 0, k * ROWS:(k + 1) * ROWS], h1[:ROWS, k * P:(k + 1) * P],
                                             ident[:ROWS, :ROWS])
                mm.then_inc(h1t_done, 1)

            def attend(g, ahead):
                if ahead is not None:
                    pe.wait_ge(sim_sb, ahead * 2 + 2)
                pe.wait_ge(attn_ready, g + 1)
                for s in range(4):
                    bank = (ps_g[:, s] if s < 2 else ps_t[:, s - 2])
                    for i in range(4):
                        mm = nc.tensor.transpose(bank[:ROWS, i * ROWS:(i + 1) * ROWS], attn[:ROWS, 4 * s + i],
                                                 ident[:ROWS, :ROWS])
                    mm.then_inc(at_done, 1)
                pe.wait_ge(v_ready, g * 2 + 2)
                for half in range(2):
                    for odd in range(2):
                        for h in range(HB * half + odd, HB * (half + 1), 2):
                            if odd == 0 and h % 4 == 0:
                                pe.wait_ge(at_sb, g * 4 + h // 4 + 1)
                            f = h // 2
                            mm = nc.tensor.matmul(ps_e[odd * DH:odd * DH + DH, half,
                                                       f % 4 * ROWS:(f % 4 + 1) * ROWS],
                                                  v_sb[:ROWS, h * DH:h * DH + DH], attnT[:ROWS, h],
                                                  start=True, stop=True)
                    mm.then_inc(o_done, 1)
                if first(g):
                    pe.wait_ge(w_o, 32)
                for f in range(FT):
                    if f % 4 == 0:
                        pe.wait_ge(ot_sb, g * 2 + f // 4 + 1)
                    mm = nc.tensor.matmul(ps_s[:ROWS, :EMB], oT[:, f], wout_sb[:, f, :],
                                          start=(f == 0), stop=(f == FT - 1))
                mm.then_inc(proj_done, 1)

            def ffn(f, after, ahead):
                pe.wait_ge(v_ready, after * 2 + 2)
                pe.wait_ge(h1t_sb, f + 1)
                for k in range(KE):
                    mm = nc.tensor.matmul(ps_s[:ROWS, :NEXP], h1T[:, k], rw_sb[:, k, :],
                                          start=(k == 0), stop=(k == KE - 1))
                mm.then_inc(rout_done, 1)
                last = isinstance(f, int) and f == G - 1
                pe.wait_ge(ht_sb, after + 1)

                def gate_up(i):
                    for k in range(KE):
                        mm = nc.tensor.matmul(ps_g[:ROWS, (i + 1) % 2], h1T[:, k], sgu_sb[:, i, k],
                                              start=(k == 0), stop=(k == KE - 1))
                    mm.then_inc(gu_done, 1)

                gate_up(0)
                gate_up(1)
                if last:
                    rank(f)
                    count()
                if ahead is not None:
                    qk(ahead, 0)
                for i in range(NFF):
                    pe.wait_ge(hid_ready, f * NFF + i + 1)
                    for k in range(KE):
                        mm = nc.tensor.transpose([ps_t[:, 0], ps_s][i][:, k * ROWS:(k + 1) * ROWS],
                                                 hid[:ROWS, i % 2, k * P:(k + 1) * P], ident[:ROWS, :ROWS])
                    mm.then_inc(hidt_done, 1)
                    if ahead is not None and i == NFF - 1:
                        qk(ahead, 1)
                for i in range(NFF):
                    pe.wait_ge(hidt_sb, f * NFF + i + 1)
                    if i == 0:
                        pe.wait_ge(sum_read, f + 1)
                    for k in range(KE):
                        mm = nc.tensor.matmul(ps_acc[:ROWS, :EMB], hidT[:, i % 2, k, :ROWS], sdown_sb[:, i * KE + k],
                                              start=(i == 0 and k == 0), stop=(i == NFF - 1 and k == KE - 1))
                mm.then_inc(ffn_done, 1)
                if ahead is not None:
                    qk(ahead, 2)
                    qk(ahead, 3)
                if not last:
                    rank(f)

            def count():
                pe.wait_ge(slots_ready, G)
                nc.tensor.matmul(ps_s[:, EMB:EMB + NEXP], ones[:ROWS, :], earlier[:ROWS], start=True, stop=True
                                 ).then_inc(counted, 1)

            def rank(f):
                pe.wait_ge(chosen_ready, f + 1)
                nc.tensor.matmul(ps_s[:ROWS, EMB:EMB + NEXP], earlier_than[:ROWS, :ROWS], chosen[:ROWS],
                                 start=True, stop=False)
                nc.tensor.matmul(ps_s[:ROWS, EMB:EMB + NEXP], ones[:ROWS, :ROWS], earlier[:ROWS],
                                 start=False, stop=True).then_inc(rank_done, 1)

            pe.wait_ge(w_tok, 16)
            pe.wait_ge(consts, N_CONSTS)
            for s, bank in enumerate([ps_g[:, 0], ps_g[:, 1], ps_t[:, 0]]):
                for j in range(2):
                    for m in range(KE):
                        mm = nc.tensor.transpose(bank[:, j * EMB + m * P:j * EMB + m * P + P],
                                                 w_nat[:, m, (2 * s + j) * P:(2 * s + j + 1) * P], ident[:])
                mm.then_inc(setup_t, 1)
            pe.wait_ge(w_small, 80)
            for m in range(KE):
                mm = nc.tensor.transpose(ps_t[:, 1, m * (TOK + 2):(m + 1) * (TOK + 2)],
                                         pe_nat[:, m * P:(m + 1) * P], ident[:TOK + 2, :TOK + 2])
            mm.then_inc(setup_t, 1)
            pe.wait_ge(setup_sb, 3)
            pe.wait_ge(tables, 8)
            pe.wait_ge(zeroed, 3)

            def before(t, ahead):
                score(t)
                v_part(t, 0)
                if not first(t):
                    attend(t - 1, t)
                cope_tables(t)
                if ahead is not None:
                    patches(ahead)
                if first(t):
                    pe.wait_ge(sim_sb, 2)
                v_part(t, 1)
                h_by_tokens(t)
                if not first(t):
                    normed(t - 1)
                if ahead is not None:
                    embed(ahead)

            patches(0)
            embed(0)
            for part in range(4):
                qk(0, part)
            before(0, 1)
            for part in range(4):
                qk(1, part)
            before(1, 2)
            pe.wait_ge(w_ffn, N_W_FFN)
            with pe.Fori(2, G - 1) as t:
                ffn(t - 2, t - 1, t)
                before(t, t + 1)
            ffn(G - 3, G - 2, G - 1)
            before(G - 1, None)
            ffn(G - 2, G - 1, None)
            attend(G - 1, None)
            normed(G - 1)
            ffn(G - 1, G - 1, None)

            x_banks = [ps_s, ps_acc]

            def transpose_x(t, turn, b):
                pe.wait_ge(tile_x[b], turn * 16 + 16)
                for k in range(KE):
                    mm = nc.tensor.transpose(x_banks[b % 2][:, k * P:(k + 1) * P], xg[:, b, k * P:(k + 1) * P],
                                             ident[:])
                mm.then_inc(tile_xt, 1)

            def experts(four):
                named = nc.tensor.value_load(tile_experts[0:1, bass.ds(four, 1)], min_val=0,
                                             max_val=NEXP ** AT_ONCE - 1)
                of = []
                for n in range(AT_ONCE):
                    of.append(nc.tensor.snap(named >> (3 * n) & (NEXP - 1)))
                return of

            def gate_up_tile(t, i, e):
                pe.wait_ge(tile_xt_sb, t + 1)
                for k in range(KE):
                    mm = nc.tensor.matmul(ps_g[:, i], xgT[:, i, k],
                                          gu_sb[:, bass.ds(e, 1), k].rearrange("p o j f -> p (o j f)"),
                                          start=(k == 0), stop=(k == KE - 1))
                mm.then_inc(tile_gu, 1)

            def tile(turn, b, ahead, e, e_ahead):
                t, i = turn * 4 + b, b % 2
                pe.wait_ge(tile_hid, t + 1)
                for k in range(KE):
                    mm = nc.tensor.transpose(ps_t[:, i, k * P:(k + 1) * P], hid[:, i, k * P:(k + 1) * P], ident[:])
                mm.then_inc(tile_hidt, 1)
                if ahead >= 3:
                    transpose_x(t + 3, turn + (b + 3) // 4, (b + 3) % 4)
                if ahead >= 2:
                    gate_up_tile(t + 2, i, e_ahead)
                pe.wait_ge(tile_hidt_sb, t + 1)
                for k in range(KE):
                    mm = nc.tensor.matmul(ps_e[:, i, :EMB], hidT[:, i, k],
                                          down_sb[:, bass.ds(e, 1), k].rearrange("p o f -> p (o f)"),
                                          start=(k == 0), stop=(k == KE - 1))
                mm.then_inc(tile_y, 1)

            pe.wait_ge(w_exp, N_W_EXP)
            pe.wait_ge(tiles_ready, 1)
            transpose_x(0, 0, 0)
            pe.wait_ge(sum_read, G + 1)
            transpose_x(1, 0, 1)
            of = experts(0)
            gate_up_tile(0, 0, of[0])
            transpose_x(2, 0, 2)
            gate_up_tile(1, 1, of[1])
            with pe.Fori(0, NT // 4 - 1) as four:
                of = experts(four)
                for b in range(4):
                    tile(four, b, 3, of[b], of[b + 2])
            of = experts(NT // 4 - 1) + [None, None]
            for n in range(6):
                t = NT - 6 + n
                tile(t // 4, t % 4, min(3, NT - 1 - t), of[n], of[n + 2])

        @block.scalar
        def _(act):
            def embed(g):
                for half, bank in enumerate([ps_s, ps_acc]):
                    act.wait_ge(xt_done, g * 2 + half + 1)
                    nc.scalar.copy(patT[:, half], bank[:, :NPH * XR].rearrange("p (c n) -> p c n", n=XR)
                                   ).then_inc(xt_sb, 1)

            def qk(g, s):
                bank = [ps_t[:, 1], ps_g[:, 0], ps_g[:, 1], ps_t[:, 0]][s]
                act.wait_ge(qk_done, g * 4 + s + 1)
                src = bank[:, :4 * ROWS].rearrange("p (f r) -> p f r", f=4)
                if s < 2:
                    fs = slice(4 * s, 4 * s + 4)
                    nc.scalar.copy(qBD[:DH, fs, 0], src[:DH])
                    nc.scalar.copy(qBD[DH:, fs, 1], src[DH:])
                    nc.scalar.copy(qT[:, fs], src).then_inc(qk_sb, 1)
                else:
                    nc.scalar.copy(kT[:, 4 * (s - 2):4 * (s - 2) + 4], src).then_inc(qk_sb, 1)

            def score(g):
                for s, banks in enumerate([ps_g, ps_t]):
                    act.wait_ge(sim_done, g * 2 + s + 1)
                    if not first(g):
                        act.wait_ge(logits, g)
                    nc.scalar.copy(split(simS, 0, TOK)[:, 2 * s:2 * s + 2],
                                   banks[:ROWS, :, :4 * ROWS].rearrange("p k (h r) -> p k h r", h=4)[:, :, :, :TOK]
                                   ).then_inc(sim_first, 1)

            def score_tanh(g):
                act.wait_ge(sim_sb, g * 2 + 2)
                nc.scalar.activation(th[:ROWS], simS[:ROWS], ACT.Tanh, scale=0.5 * SCALE).then_inc(tanh_sb, 1)

            def v_part(g, s):
                act.wait_ge(v_done, g * 2 + s + 1)
                nc.scalar.copy(v_sb[:ROWS, 512 * s:512 * s + 512], [ps_acc, ps_g[:, 1]][s][:ROWS]
                               ).then_inc(v_ready, 1)

            def h_by_tokens(g):
                act.wait_ge(ht_done, g + 1)
                if not first(g):
                    act.wait_ge(res1_done, g)
                nc.scalar.copy(htok[:ROWS], ps_t[:ROWS, 1, :EMB]).then_inc(ht_sb, 1)

            def normed(f):
                act.wait_ge(h1t_done, f + 1)
                nc.scalar.copy(h1T[:], ps_g[:, 0, :KE * ROWS].rearrange("p (k r) -> p k r", k=KE)
                               ).then_inc(h1t_sb, 1)

            def attend(g):
                for s in range(2):
                    act.wait_ge(o_done, g * 2 + s + 1)
                    nc.scalar.copy(oT[:, 4 * s:4 * s + 4],
                                   ps_e[:, s, :4 * ROWS].rearrange("p (f r) -> p f r", f=4)).then_inc(ot_sb, 1)

            def softmax_exp(g):
                act.wait_ge(logits, g + 1)
                nc.scalar.activation(ex[:ROWS], lg[:ROWS], ACT.Exp).then_inc(exp_ready, 1)

            def spread(g):
                act.wait_ge(weights, g + 1)
                nc.scalar.copy(attn[:ROWS], lg[:ROWS].unsqueeze(2).to_broadcast([ROWS, HEADS, TPG, TOK])
                               ).then_inc(attn_ready, 1)

            def ffn(f, ahead):
                def gate_tanh(i):
                    act.wait_ge(gu_done, f * NFF + i + 1)
                    nc.scalar.activation(thg[:ROWS, i % 2], ps_g[:ROWS, (i + 1) % 2, :FF], ACT.Tanh, scale=0.5
                                         ).then_inc(thg_ready, 1)

                gate_tanh(0)
                act.wait_ge(rlg_ready, f + 1)
                nc.scalar.activation(rexp[:ROWS], rlg[:ROWS], ACT.Exp, accum_out=rsum[:ROWS]
                                     ).then_inc(rexp_ready, 1)
                gate_tanh(1)
                if ahead is not None:
                    qk(ahead, 0)
                for i in range(NFF):
                    act.wait_ge(hidt_done, f * NFF + i + 1)
                    nc.scalar.copy(hidT[:, i % 2, :, :ROWS],
                                   [ps_t[:, 0], ps_s][i][:, :KE * ROWS].rearrange("p (k r) -> p k r", k=KE)
                                   ).then_inc(hidt_sb, 1)
                if ahead is not None:
                    for part in range(1, 4):
                        qk(ahead, part)

            act.wait_ge(setup_t, 3)
            for s, bank in enumerate([ps_g[:, 0], ps_g[:, 1], ps_t[:, 0]]):
                nc.scalar.copy(tokT[:, 2 * s:2 * s + 2], bank.rearrange("p (j e) -> p j e", j=2)
                               ).then_inc(setup_sb, 1)
            act.wait_ge(zeroed, 3)

            def before(t, ahead):
                if not first(t):
                    softmax_exp(t - 1)
                score(t)
                if not first(t):
                    spread(t - 1)
                score_tanh(t)
                if not first(t):
                    attend(t - 1)
                v_part(t, 0)
                if ahead is not None:
                    embed(ahead)
                v_part(t, 1)
                h_by_tokens(t)
                if not first(t):
                    normed(t - 1)

            embed(0)
            for part in range(4):
                qk(0, part)
            before(0, 1)
            for part in range(4):
                qk(1, part)
            before(1, 2)
            with act.Fori(2, G - 1) as t:
                ffn(t - 2, t)
                before(t, t + 1)
            ffn(G - 3, G - 1)
            before(G - 1, None)
            ffn(G - 2, None)
            softmax_exp(G - 1)
            spread(G - 1)
            attend(G - 1)
            normed(G - 1)
            ffn(G - 1, None)

            x_banks = [ps_s, ps_acc]

            def x_in_sbuf(t, i):
                act.wait_ge(tile_xt, t + 1)
                nc.scalar.copy(xgT[:, i], x_banks[i][:, :EMB].rearrange("p (k r) -> p k r", k=KE)
                               ).then_inc(tile_xt_sb, 1)

            def tanh_tile(t, i):
                act.wait_ge(tile_gu, t + 1)
                nc.scalar.activation(thg[:, i], ps_g[:, i, :FF], ACT.Tanh, scale=0.5).then_inc(tile_tanh, 1)

            def tile(t, i, ahead):
                act.wait_ge(tile_hidt, t + 1)
                nc.scalar.copy(hidT[:, i], ps_t[:, i, :EMB].rearrange("p (k r) -> p k r", k=KE)
                               ).then_inc(tile_hidt_sb, 1)
                if ahead >= 3:
                    x_in_sbuf(t + 3, 1 - i)
                if ahead >= 2:
                    tanh_tile(t + 2, i)

            x_in_sbuf(0, 0)
            x_in_sbuf(1, 1)
            tanh_tile(0, 0)
            act.wait_ge(tile_gu, 1)
            x_in_sbuf(2, 0)
            tanh_tile(1, 1)
            with act.Fori(0, NT // 2 - 2) as pair:
                for i in range(2):
                    tile(pair * 2 + i, i, 3)
            for t in range(NT - 4, NT):
                tile(t, t % 2, min(3, NT - 1 - t))

            def store(g, row, b, lo):
                act.wait_ge(out_ready, g + 1)
                n = (ROWS - lo) // 16 * 16
                act.dma_start(out_rows[bass.ds(row, n), :], outc[lo:lo + n, b]).then_inc(stored[b], 16)
                act.dma_start(out_rows[bass.ds(row + n, ROWS - lo - n), :], outc[lo + n:ROWS, b]
                              ).then_inc(stored[b], 16)

            with act.Fori(0, G // NB) as four:
                for b in range(NB):
                    g = four * NB + b
                    store(g, g * ROWS, b, 0)
            store(G - 2, (G - 2) * ROWS, (G - 2) % NB, 0)
            done = (G - 1) * TPG
            store(G - 1, done * TOK, (G - 1) % NB, (done - IMGS + TPG) * TOK)
            for b in range(NB):
                act.wait_ge(stored[b], 32 * -(-(G - b) // NB))

        @block.vector
        def _(dve):
            class Steps:

                def __init__(self, sem, per):
                    self.sem, self.per, self.n = sem, per, 0

                def did(self, ins):
                    ins.then_inc(self.sem, 1)
                    self.n += 1

                def settle(self, g):
                    dve.wait_ge(self.sem, g * self.per + self.n)

                def end(self):
                    assert self.n == self.per, (self.n, self.per)
                    self.n = 0

            A = Steps(dve_attn, DVE_ATTN)
            S = Steps(dve_soft, DVE_SOFT)
            F = Steps(dve_ffn, DVE_FFN)
            V = nc.vector

            def embed(g):
                dve.wait_ge(emb_done, g + 1)
                for m in range(KE):
                    src = ps_t[:, 0, m * NPAT:(m + 1) * NPAT].rearrange("p (c b r) -> p c b r", c=NPH, b=TPG)
                    dst = hT[:, m, :, 1:].rearrange("p b (r c) -> p c b r", c=NPH)
                    pos = posb[:, m, 1:].rearrange("p (r c) -> p c r", c=NPH).unsqueeze(2).to_broadcast(
                        [P, NPH, TPG, NPH])
                    V.tensor_tensor(dst, src, pos, ALU.add).then_inc(hT_ready, 1)

            table = ps_e[:ROWS, :, :HB * SLP].rearrange("p s (h a) -> p s h a", a=SLP)

            def flat(t):
                return t[:ROWS].rearrange("p h a -> p (h a)")

            def scores(g):
                for s, banks in enumerate([ps_g, ps_t]):
                    dve.wait_ge(sim_first, g * 2 + s + 1)
                    src = banks[:ROWS, :, :4 * ROWS].rearrange("p k (h r) -> p k h r", h=4)
                    dst = split(simS, 0, TOK)[:, 2 * s:2 * s + 2]
                    for b in range(1, TPG):
                        apart(dve)
                        own = own_img[:ROWS, b:b + 1].unsqueeze(2).unsqueeze(3).to_broadcast([ROWS, 2, 4, TOK])
                        ins = V.copy_predicated(dst, own, src[:, :, :, b * TOK:(b + 1) * TOK])
                        if b < TPG - 1:
                            A.did(ins)
                            A.settle(g)
                        else:
                            ins.then_inc(sim_sb, 1)

            def cope(g, part):
                if part == 0:
                    dve.wait_ge(tanh_sb, g + 1)
                    A.did(V.tensor_scalar(gate[:ROWS, :, 1:1 + TOK], th[:ROWS], -0.5, 0.5, ALU.mult, ALU.add))
                if part == 1:
                    A.settle(g)
                    A.did(V.tensor_tensor_scan(flat(u)[:, ::-1], flat(scan_keep)[:, ::-1], flat(gate)[:, ::-1],
                                               0.0, ALU.mult, ALU.add))
                if part == 2:
                    A.settle(g)
                    A.did(V.tensor_scalar(flat(rr), flat(u), RNE, -RNE, ALU.add, ALU.add))
                    A.settle(g)
                    A.did(V.tensor_tensor(flat(up), flat(u), flat(rr), ALU.is_gt))
                    A.settle(g)
                    A.did(V.tensor_tensor(flat(dI), flat(rr), flat(up), ALU.add))
                if part == 3:
                    A.settle(g)
                    A.did(V.tensor_scalar(flat(dE), flat(dI), 62, None, ALU.bitwise_and))
                    for n, d in enumerate(SHIFTS):
                        ins = V.tensor_scalar(bit[:ROWS, n].rearrange("p h a -> p (h a)"), flat(dI), d, None,
                                              ALU.bitwise_and)
                    A.did(ins)
                    A.settle(g)
                    A.did(V.tensor_tensor(flat(q), flat(u), flat(dE), ALU.subtract))
                if part == 4:
                    dve.wait_ge(cope_done, g + 1)
                    for n, d in enumerate(SHIFTS):
                        A.settle(g)
                        apart(dve)
                        A.did(V.copy_predicated(table[:, :, :, 0:SL - d], halves(bit[:, n], 0, SL - d),
                                                table[:, :, :, d:SL]))
                if part == 5:
                    A.settle(g)
                    A.did(V.tensor_scalar(qpos[:ROWS], q[:ROWS, :, 1:1 + TOK], 0.0, None, ALU.is_gt))
                    A.did(V.tensor_copy(halves(nb, 0, TOK), table[:, :, :, 0:TOK]))
                    A.settle(g)
                    apart(dve)
                    A.did(V.copy_predicated(halves(nb, 0, TOK), halves(qpos, 0, TOK), table[:, :, :, 2:2 + TOK]))
                    A.did(V.tensor_scalar(flat(q).bitcast(U32), flat(q).bitcast(U32), 0x7FFFFFFF, None,
                                          ALU.bitwise_and))
                if part == 6:
                    centre = table[:, :, :, 1:1 + TOK]
                    A.settle(g)
                    A.did(V.tensor_tensor(halves(nb, 0, TOK), halves(nb, 0, TOK), centre, ALU.subtract))
                    A.settle(g)
                    A.did(V.tensor_tensor(nb[:ROWS], q[:ROWS, :, 1:1 + TOK], nb[:ROWS], ALU.mult))
                    A.settle(g)
                    A.did(V.tensor_tensor(halves(nb, 0, TOK), halves(nb, 0, TOK), centre, ALU.add))
                if part == 7:
                    A.settle(g)
                    A.did(V.scalar_tensor_tensor(nb[:ROWS], simS[:ROWS], SCALE, nb[:ROWS], ALU.mult, ALU.add))
                    A.settle(g)
                    A.did(V.tensor_reduce(mx[:ROWS], nb[:ROWS], AX_X, ALU.max))
                    A.settle(g)
                    V.tensor_tensor(lg[:ROWS], nb[:ROWS], mx[:ROWS].unsqueeze(2).to_broadcast([ROWS, HEADS, TOK]),
                                    ALU.subtract).then_inc(logits, 1)
                    A.end()

            def attention(g):
                keep = same_img[:ROWS].rearrange("p b j -> p (b j)").unsqueeze(1).to_broadcast([ROWS, 4, ROWS])
                for s in range(4):
                    bank = (ps_g[:, s] if s < 2 else ps_t[:, s - 2])
                    dve.wait_ge(at_done, g * 4 + s + 1)
                    V.tensor_tensor(attnT[:ROWS, 4 * s:4 * s + 4],
                                    bank[:ROWS, :4 * ROWS].rearrange("p (h r) -> p h r", h=4), keep, ALU.mult
                                    ).then_inc(at_sb, 1)

            def softmax_norm(g):
                dve.wait_ge(exp_ready, g + 1)
                S.did(V.tensor_reduce(den[:ROWS], ex[:ROWS], AX_X, ALU.add))
                S.settle(g)
                S.did(V.reciprocal(rden[:ROWS], den[:ROWS]))
                S.settle(g)
                V.tensor_tensor(lg[:ROWS], ex[:ROWS], rden[:ROWS].unsqueeze(2).to_broadcast([ROWS, HEADS, TOK]),
                                ALU.mult).then_inc(weights, 1)

            def norm1(g):
                dve.wait_ge(proj_done, g + 1)
                dve.wait_ge(htok_ready, g + 1)
                V.tensor_tensor(res1[:ROWS], ps_s[:ROWS, :EMB], htok[:ROWS], ALU.add).then_inc(res1_done, 1)
                dve.wait_ge(res1_done, g + 1)
                S.did(V.bn_stats(st1[:ROWS], res1[:ROWS]))
                S.settle(g)
                apart(dve)
                S.did(V.bn_aggr(mv1[:ROWS], st1[:ROWS]))
                S.settle(g)
                V.tensor_scalar(ve1[:ROWS], mv1[:ROWS, 1:2], EPS, None, ALU.add).then_inc(var1, 1)
                if not first(g):
                    dve.wait_ge(h1_stored, g * 16 * TOPK)
                    dve.wait_ge(h1t_done, g)
                dve.wait_ge(rstd1, g + 1)
                V.tensor_scalar(h1[:ROWS], res1[:ROWS], mv1[:ROWS, 0:1], rs1[:ROWS], ALU.subtract, ALU.mult
                                ).then_inc(h1_ready, 1)
                S.end()

            def router(f, part):
                if part == 0:
                    dve.wait_ge(rout_done, f + 1)
                    F.did(V.tensor_reduce(rmax[:ROWS], ps_s[:ROWS, :NEXP], AX_X, ALU.max))
                    F.settle(f)
                    V.tensor_scalar(rlg[:ROWS], ps_s[:ROWS, :NEXP], rmax[:ROWS], None, ALU.subtract
                                    ).then_inc(rlg_ready, 1)
                if part == 1:
                    dve.wait_ge(rexp_ready, f + 1)
                    F.did(V.reciprocal(rinv[:ROWS], rsum[:ROWS]))
                    F.settle(f)
                    F.did(V.tensor_scalar(rsc[:ROWS], rexp[:ROWS], rinv[:ROWS], None, ALU.mult))
                    F.settle(f)
                    apart(dve)
                    F.did(V.max(top[:ROWS], rsc[:ROWS]))
                    F.settle(f)
                    apart(dve)
                    F.did(V.max_index(topi[:ROWS], top[:ROWS], rsc[:ROWS]))
                    F.settle(f)
                    F.did(V.tensor_copy(topf[:ROWS], topi[:ROWS]))
                    F.settle(f)
                    F.did(V.tensor_scalar(c1[:ROWS], iota8[:ROWS], topf[:ROWS, 0:1], None, ALU.is_equal))
                    F.did(V.tensor_scalar(c2[:ROWS], iota8[:ROWS], topf[:ROWS, 1:2], None, ALU.is_equal))
                    F.settle(f)
                    V.tensor_tensor(chosen[:ROWS], c1[:ROWS], c2[:ROWS], ALU.add).then_inc(chosen_ready, 1)

            def hidden_sum(f):
                dve.wait_ge(rec_stored, f * 16 + 1)
                dve.wait_ge(ffn_done, f + 1)
                V.tensor_tensor(rec[:ROWS, :EMB], ps_acc[:ROWS, :EMB], h1[:ROWS], ALU.add).then_inc(sum_read, 1)
                dve.wait_ge(sum_read, f + 2)
                V.tensor_copy(rec[:ROWS, EMB:EMB + TOPK], top[:ROWS, :TOPK]).then_inc(rec_ready, 1)

            def slots(f):
                dve.wait_ge(ids_left, f + 1)
                dve.wait_ge(rank_done, f + 1)
                F.did(V.tensor_tensor(slot8[:ROWS], ps_s[:ROWS, EMB:EMB + NEXP], slot0[:ROWS], ALU.add))
                F.did(V.tensor_tensor(earlier[:ROWS], earlier[:ROWS], chosen[:ROWS], ALU.add))
                F.did(V.tensor_copy(ids[:ROWS, 0:1], idf[:ROWS]))
                F.did(V.tensor_scalar(ids[:ROWS, 1:2], idf[:ROWS], float(TOKENS), None, ALU.add))
                F.settle(f)
                F.did(V.tensor_tensor(pick[:ROWS, 0], c1[:ROWS], slot8[:ROWS], ALU.mult))
                F.did(V.tensor_tensor(pick[:ROWS, 1], c2[:ROWS], slot8[:ROWS], ALU.mult))
                F.did(V.tensor_scalar(idf[:ROWS], idf[:ROWS], float(ROWS), None, ALU.add))
                F.settle(f)
                F.did(V.tensor_reduce(slotf[:ROWS], pick[:ROWS], AX_X, ALU.add))
                F.settle(f)
                V.tensor_copy(slotu[:ROWS], slotf[:ROWS]).then_inc(slots_ready, 1)

            def hidden(f, i):
                bank = ps_g[:ROWS, (i + 1) % 2]
                dve.wait_ge(thg_ready, f * NFF + i + 1)
                F.did(V.scalar_tensor_tensor(sg[:ROWS, i % 2], thg[:ROWS, i % 2], 1.0, bank[:, :FF],
                                             ALU.add, ALU.mult))
                F.settle(f)
                V.scalar_tensor_tensor(hid[:ROWS, i % 2], sg[:ROWS, i % 2], 0.5, bank[:, FF:],
                                       ALU.mult, ALU.mult).then_inc(hid_ready, 1)

            def tiles():
                W = Steps(dve_tab, 0)
                dve.wait_ge(counted, 1)
                tiles_of, through, one8 = cnt[:, 0], cnt[:, 1], cnt[:, 2]
                W.did(V.tensor_scalar(tiles_of, ps_s[:, EMB:EMB + NEXP], (P - 1) / 2, 1.0 / P, ALU.add, ALU.mult))
                W.did(V.memset(one8, 1.0))
                W.settle(0)
                W.did(V.tensor_scalar(tiles_of, tiles_of, RNE, -RNE, ALU.add, ALU.add))
                W.settle(0)
                W.did(V.tensor_tensor_scan(through, one8, tiles_of, 0.0, ALU.mult, ALU.add))
                W.settle(0)
                by_tile = [P, NT, NEXP]
                W.did(V.tensor_tensor(past[:], tile_no[:].unsqueeze(2).to_broadcast(by_tile),
                                      through.unsqueeze(1).to_broadcast(by_tile), ALU.is_ge))
                W.settle(0)
                W.did(V.tensor_reduce(tl[:, 0], past[:], AX_X, ALU.add))
                W.settle(0)
                W.did(V.tensor_tensor(past[:], past[:], tiles_of.unsqueeze(1).to_broadcast(by_tile), ALU.mult))
                W.settle(0)
                W.did(V.tensor_reduce(tl[:, 1], past[:], AX_X, ALU.add))
                W.settle(0)
                W.did(V.tensor_tensor(tl[:, 1], tile_no[:], tl[:, 1], ALU.subtract))
                W.did(V.tensor_scalar(tl[:, 2], tl[:, 0], float(CAP), None, ALU.mult))
                W.settle(0)
                W.did(V.scalar_tensor_tensor(tl[:, 2], tl[:, 1], float(P), tl[:, 2], ALU.mult, ALU.add))
                W.did(V.tensor_scalar(tl[:, 0], tl[:, 0], float(NEXP - 1), None, ALU.min))
                W.settle(0)
                W.did(V.tensor_copy(tile_slot[:], tl[:, 2]))
                of_place = [tl[:, 0, n:n + NT - AT_ONCE + 1:4] for n in range(AT_ONCE)]
                W.did(V.tensor_copy(names[:], of_place[-1]))
                for n in range(AT_ONCE - 2, -1, -1):
                    W.settle(0)
                    W.did(V.scalar_tensor_tensor(names[:], names[:], float(NEXP), of_place[n], ALU.mult, ALU.add))
                W.settle(0)
                W.did(V.tensor_copy(tile_experts[:], names[:]))
                W.settle(0)
                V.nop().then_inc(tiles_ready, 1)

            def ffn(f, g):
                if isinstance(f, int) and f == G - 1:
                    router(f, 0)
                    router(f, 1)
                    slots(f)
                    tiles()
                    hidden(f, 0)
                    hidden(f, 1)
                    hidden_sum(f)
                    F.end()
                    return

                def part(n):
                    if g is not None:
                        cope(g, n)

                router(f, 0)
                hidden(f, 0)
                router(f, 1)
                hidden(f, 1)
                part(6)
                hidden_sum(f)
                part(7)
                slots(f)
                F.end()

            def middle(t):
                softmax_norm(t - 1)
                scores(t)
                cope(t, 0)
                attention(t - 1)
                for part in range(1, 4):
                    cope(t, part)
                norm1(t - 1)
                cope(t, 4)
                cope(t, 5)

            for free in (sum_read, rec_stored):
                dve.nop().then_inc(free, 1)

            dve.wait_ge(setup_t, 4)
            dve.wait_ge(zeroed, 3)
            V.tensor_copy(posT[:], ps_t[:, 1, :KE * (TOK + 2)].rearrange("p (m t) -> p m t", m=KE)
                          ).then_inc(tables, 1)
            dve.wait_ge(tables, 1)
            for m in range(KE):
                V.tensor_scalar(posb[:, m, 1:], posT[:, m, 1:TOK], posT[:, m, TOK:TOK + 1], None, ALU.add
                                ).then_inc(tables, 1)
                V.tensor_tensor(hT[:, m, :, 0:1], posT[:, m, 0:1].unsqueeze(1).to_broadcast([P, TPG, 1]),
                                posT[:, m, TOK + 1:].unsqueeze(1).to_broadcast([P, TPG, 1]), ALU.add
                                ).then_inc(tables, 1)
            for h in range(2):
                part = slice(DH * h, DH * h + DH)
                V.tensor_copy(cope_bd[part, h, :SL], cope_nat[part, SL - 1::-1]).then_inc(tables, 1)
            dve.wait_ge(consts, N_CONSTS)
            V.tensor_copy(own_img[:], same_img[:, :, 0]).then_inc(tables, 1)
            dve.wait_ge(tables, 8)

            embed(0)
            scores(0)
            for part in range(4):
                cope(0, part)
            embed(1)
            for part in range(4, 8):
                cope(0, part)
            middle(1)
            embed(2)

            with dve.Fori(2, G - 1) as t:
                ffn(t - 2, t - 1)
                middle(t)
                embed(t + 1)
            ffn(G - 3, G - 2)
            middle(G - 1)
            ffn(G - 2, G - 1)
            softmax_norm(G - 1)
            attention(G - 1)
            norm1(G - 1)
            ffn(G - 1, None)

            def hidden_tile(t, i):
                dve.wait_ge(tile_tanh, t + 1)
                V.scalar_tensor_tensor(sg[:, i], thg[:, i], 1.0, ps_g[:, i, :FF], ALU.add, ALU.mult
                                       ).then_inc(dve_tile, 1)
                dve.wait_ge(dve_tile, t + 1)
                V.scalar_tensor_tensor(hid[:, i], sg[:, i], 0.5, ps_g[:, i, FF:], ALU.mult, ALU.mult
                                       ).then_inc(tile_hid, 1)

            def y_tile(t, turn, b):
                if turn is not None:
                    dve.wait_ge(tile_stored[(b + 2) % 4], turn * 16)
                dve.wait_ge(tile_y, t + 1)
                V.tensor_copy(y_sb[:, b % 2], ps_e[:, b % 2, :EMB]).then_inc(tile_y_sb, 1)

            hidden_tile(0, 0)
            for t in range(4):
                hidden_tile(t + 1, (t + 1) % 2)
                y_tile(t, 1 if t >= 2 else None, t)
            with dve.Fori(1, NT // 4) as four:
                for b in range(4):
                    hidden_tile(four * 4 + b + 1, (b + 1) % 2)
                    y_tile(four * 4 + b, four + b // 2, b)
            hidden_tile(NT - 1, 1)
            y_tile(NT - 2, NT // 4, 0)
            y_tile(NT - 1, NT // 4, 1)

            L = Steps(dve_last, 8)

            def norm2(pair, turn, b, n):
                if n == 0:
                    dve.wait_ge(rstd2, pair + 1)
                if not first(turn):
                    dve.wait_ge(stored[b + n], turn * 32)
                V.tensor_scalar(outc[:ROWS, b + n], resc[:ROWS, b + n], mvc[:ROWS, b + n, 0:1],
                                rsc2[:ROWS, bass.ds(pair * 2 + n, 1)], ALU.subtract, ALU.mult).then_inc(out_ready, 1)

            def last_pass(pair, turn, b, before):
                for c in (b, b + 1):
                    dve.wait_ge(rec_in[c], (turn + 1) * 16 * 2)
                    L.did(V.scalar_tensor_tensor(resc[:ROWS, c], yc[:ROWS, c, 0], recc[:ROWS, c, EMB:EMB + 1],
                                                 recc[:ROWS, c, :EMB], ALU.mult, ALU.add))
                if before is not None:
                    norm2(*before, 0)
                L.settle(pair)
                for c in (b, b + 1):
                    L.did(V.scalar_tensor_tensor(resc[:ROWS, c], yc[:ROWS, c, 1], recc[:ROWS, c, EMB + 1:EMB + 2],
                                                 resc[:ROWS, c], ALU.mult, ALU.add))
                if before is not None:
                    norm2(*before, 1)
                L.settle(pair)
                apart(dve)
                for c in (b, b + 1):
                    L.did(V.bn_stats(stc[:ROWS, c], resc[:ROWS, c]))
                L.settle(pair)
                apart(dve)
                for c in (b, b + 1):
                    L.did(V.bn_aggr(mvc[:ROWS, c], stc[:ROWS, c]))
                L.settle(pair)
                V.tensor_scalar(vec[:ROWS, bass.ds(pair * 2, 2)], mvc[:ROWS, b:b + 2, 1], EPS, None, ALU.add
                                ).then_inc(var2, 1)
                L.end()

            last_pass(0, 0, 0, None)
            last_pass(1, 0, 2, (0, 0, 0))
            last_pass(2, 1, 0, (1, 0, 2))
            last_pass(3, 1, 2, (2, 1, 0))
            with dve.Fori(2, G // NB) as four:
                last_pass(four * 2, four, 0, (four * 2 - 1, four - 1, 2))
                last_pass(four * 2 + 1, four, 2, (four * 2, four, 0))
            last = G // 2 - 1
            last_pass(last, G // NB, 0, (last - 1, G // NB - 1, 2))
            for n in range(2):
                norm2(last, G // NB, 0, n)


_INS = ['x', 'L0_tok_W', 'L0_tok_b', 'L0_tok_cls_token', 'L0_tok_pos_embed', 'L0_attn_Wq', 'L0_attn_Wkv',
        'L0_attn_Wout', 'L0_attn_b_out', 'L0_attn_pos_emb', 'L0_ffn_router_w', 'L0_ffn_gate_w', 'L0_ffn_up_w',
        'L0_ffn_down_w', 'L0_ffn_shared_gate_w', 'L0_ffn_shared_up_w', 'L0_ffn_shared_down_w']
_OUTS = [((64, 37, 256), 'float32')]


def kernel(**inputs):
    import numpy as _np
    import concourse.bacc as _bacc
    from concourse import mybir as _mybir
    from concourse.bass_utils import run_bass_kernel_spmd as _run

    nc = _bacc.Bacc("TRN2", target_bir_lowering=False, num_devices=1)
    arrays, args = {}, []
    for name in _INS:
        a = _np.ascontiguousarray(inputs[name])
        arrays[f"in_{name}_dram"] = a
        args.append(nc.dram_tensor(f"in_{name}_dram", a.shape, _mybir.dt.from_np(a.dtype), kind="ExternalInput").ap())
    for i, (shape, dtype) in enumerate(_OUTS):
        dt = _mybir.dt.from_np(_np.dtype(dtype))
        args.append(nc.dram_tensor(f"out_{i}_dram", shape, dt, kind="ExternalOutput").ap())
    vit_tower(nc, *args)
    r = _run(nc, [arrays], core_ids=[0])
    got = tuple(r.results[0][f"out_{i}_dram"] for i in range(len(_OUTS)))
    return got[0]
```
